# Optimizing a Trainium2 kernel written in Bass

```python
import numpy as np
import jax
import jax.numpy as jnp

def _softmax(x, axis=-1):
    return jax.nn.softmax(x, axis=axis)

def _gelu(x):
    return jax.nn.gelu(x, approximate=True)

def _silu(x):
    return jax.nn.silu(x)

def _sigmoid(x):
    return jax.nn.sigmoid(x)

def _layernorm(x, axis=-1, eps=1e-05):
    m = jnp.mean(x, axis=axis, keepdims=True)
    v = jnp.var(x, axis=axis, keepdims=True)
    return (x - m) / jnp.sqrt(v + eps)

def _scatter_add(tgt, idx, src, axis=0):
    return tgt.at[idx].add(src)

def _segment_sum(src, seg, n):
    return jax.ops.segment_sum(src, seg, n)
kernel_name = 'mk_gnn_ffn_d1_gnn_r32_0bfe18'

def setup_inputs(seed: int=0):
    np.random.seed(seed)
    _w = jnp.asarray

    def _rec_inputs():
        import jax
        import jax.numpy as jnp
        _gk = jax.random.key(seed)
        x = -0.0002117 + 1 * jax.random.normal(jax.random.fold_in(_gk, 1), (3125, 256), jnp.float32)
        src = jax.random.randint(jax.random.fold_in(_gk, 2), (50000,), 0, 3125, jnp.int32)
        dst = jnp.minimum((3125 * jax.random.uniform(jax.random.fold_in(_gk, 3), (50000,)) ** 2.0).astype(jnp.int32), 99999)
        _o = jnp.argsort(dst, stable=True)
        src = src[_o]
        dst = dst[_o]
        edge_weight = jax.random.uniform(jax.random.fold_in(_gk, 12), (50000,), jnp.float32, 0.0, 1)
        return (x, src, dst, edge_weight)
    x, src, dst, edge_weight = _rec_inputs()

    def _L0_gnn_setup():
        import jax, jax.numpy as jnp
        import numpy as np
        N_NODES = 3125
        N_EDGES = 50000
        D_FEAT = 256
        LAYERS = 3
        EPS = 1e-12

        def _spmm(vals, row, col, h, n_nodes):
            msgs = vals[:, None] * h[col]
            return jax.ops.segment_sum(msgs, row, num_segments=n_nodes, indices_are_sorted=True)

        def _l2_normalize(h):
            norm = jnp.sqrt(jnp.sum(h * h, axis=-1, keepdims=True))
            return h / jnp.maximum(norm, EPS)
        key = jax.random.key(seed)
        k1, k2, k3, k4 = jax.random.split(key, 4)
        x = jax.random.normal(k1, (N_NODES, D_FEAT), dtype=jnp.float32)
        vals = jax.random.uniform(k2, (N_EDGES,), dtype=jnp.float32)
        row = jnp.sort(jax.random.randint(k3, (N_EDGES,), 0, N_NODES, dtype=jnp.int32))
        col = jax.random.randint(k4, (N_EDGES,), 0, N_NODES, dtype=jnp.int32)
        return {'x': x, 'vals': vals, 'row': row, 'col': col}
    _L0_gnn_all = _L0_gnn_setup()
    _L0_gnn_in = {k: v for k, v in _L0_gnn_all.items() if k in ()}
    del _L0_gnn_all

    def _L0_ffn_setup():
        import jax, jax.numpy as jnp
        import numpy as np
        B, S, H, F, E, K = (8, 128, 256, 512, 16, 2)
        EPS = 1e-05
        key = jax.random.key(seed)
        ks = jax.random.split(key, 9)
        sc = 0.02
        return {'x': jax.random.normal(ks[0], (B, S, H), dtype=jnp.float32), 'gate_w': jax.random.normal(ks[1], (H, E), dtype=jnp.float32) * sc, 'gate_b': jnp.zeros((E,), dtype=jnp.float32), 'w1': jax.random.normal(ks[2], (E, H, F), dtype=jnp.float32) * sc, 'b1': jnp.zeros((E, F), dtype=jnp.float32), 'w2': jax.random.normal(ks[3], (E, F, H), dtype=jnp.float32) * sc, 'b2': jnp.zeros((E, H), dtype=jnp.float32), 'gamma': jnp.ones((H,), dtype=jnp.float32), 'beta': jnp.zeros((H,), dtype=jnp.float32)}
    _L0_ffn_all = _L0_ffn_setup()
    _L0_ffn_in = {k: v for k, v in _L0_ffn_all.items() if k in ('gate_w', 'gate_b', 'w1', 'b1', 'w2', 'b2', 'gamma', 'beta')}
    del _L0_ffn_all
    return {'x': x, 'src': src, 'dst': dst, 'edge_weight': edge_weight, 'L0_ffn_gate_w': _L0_ffn_in['gate_w'], 'L0_ffn_gate_b': _L0_ffn_in['gate_b'], 'L0_ffn_w1': _L0_ffn_in['w1'], 'L0_ffn_b1': _L0_ffn_in['b1'], 'L0_ffn_w2': _L0_ffn_in['w2'], 'L0_ffn_b2': _L0_ffn_in['b2'], 'L0_ffn_gamma': _L0_ffn_in['gamma'], 'L0_ffn_beta': _L0_ffn_in['beta']}

def reference(x, src, dst, edge_weight, L0_ffn_gate_w, L0_ffn_gate_b, L0_ffn_w1, L0_ffn_b1, L0_ffn_w2, L0_ffn_b2, L0_ffn_gamma, L0_ffn_beta):
    import jax
    import jax.numpy as jnp

    def _L0_gnn_ref(x, vals, row, col):
        import jax, jax.numpy as jnp
        import numpy as np
        N_NODES = 3125
        N_EDGES = 50000
        D_FEAT = 256
        LAYERS = 3
        EPS = 1e-12

        def _spmm(vals, row, col, h, n_nodes):
            msgs = vals[:, None] * h[col]
            return jax.ops.segment_sum(msgs, row, num_segments=n_nodes, indices_are_sorted=True)

        def _l2_normalize(h):
            norm = jnp.sqrt(jnp.sum(h * h, axis=-1, keepdims=True))
            return h / jnp.maximum(norm, EPS)
        n_nodes = x.shape[0]
        h = x
        acc = x
        for _ in range(LAYERS):
            h = _spmm(vals, row, col, h, n_nodes)
            h = _l2_normalize(h)
            acc = acc + h
        return acc / (LAYERS + 1)

    def _L0_ffn_ref(x, gate_w, gate_b, w1, b1, w2, b2, gamma, beta):
        import jax, jax.numpy as jnp
        import numpy as np
        B, S, H, F, E, K = (8, 128, 256, 512, 16, 2)
        EPS = 1e-05
        gate_logits = x @ gate_w + gate_b
        topk_vals, topk_idx = jax.lax.top_k(gate_logits, K)
        topk_w = jax.nn.softmax(topk_vals, axis=-1)
        h = jax.nn.relu(jnp.einsum('bsh,ehf->bsef', x, w1) + b1)
        expert_out = jnp.einsum('bsef,efh->bseh', h, w2) + b2
        sel = jnp.take_along_axis(expert_out, topk_idx[:, :, :, None], axis=2)
        moe = jnp.sum(topk_w[..., None] * sel, axis=2)
        y = x + moe
        mu = jnp.mean(y, axis=-1, keepdims=True)
        var = jnp.var(y, axis=-1, keepdims=True)
        return (y - mu) / jnp.sqrt(var + EPS) * gamma + beta
    x = x + _L0_gnn_ref(_layernorm(x, axis=-1), edge_weight, src, dst)
    x = x + _L0_ffn_ref(_layernorm(x, axis=-1)[None], L0_ffn_gate_w, L0_ffn_gate_b, L0_ffn_w1, L0_ffn_b1, L0_ffn_w2, L0_ffn_b2, L0_ffn_gamma, L0_ffn_beta)[0]
    return x

_drawn_inputs = setup_inputs


def setup_inputs(seed=0):
    import zlib

    import numpy as np

    out = dict(_drawn_inputs(seed))
    spreads = {'L0_ffn_gate_b': (0.0, 0.1),
     'L0_ffn_b1': (0.0, 0.792),
     'L0_ffn_b2': (0.0, 0.1),
     'L0_ffn_gamma': (1.0, 0.2),
     'L0_ffn_beta': (0.0, 0.1)}
    factors = {'edge_weight': 4.436}
    for name, (base, spread) in spreads.items():
        noise = np.random.default_rng([zlib.crc32(name.encode()), seed]).standard_normal(out[name].shape)
        drawn = base * np.exp(spread * noise) if base else spread * noise
        out[name] = jnp.asarray(drawn.astype(out[name].dtype))
    for name, factor in factors.items():
        out[name] = (out[name] * factor).astype(out[name].dtype)
    return out
```

```python
from contextlib import ExitStack

import concourse.bass as bass
from concourse import mybir

F32 = mybir.dt.float32
F32R = mybir.dt.float32r
BF16 = mybir.dt.bfloat16
I32 = mybir.dt.int32
U32 = mybir.dt.uint32
ALU = mybir.AluOpType
ACT = mybir.ActivationFunctionType
AX = mybir.AxisListType

P = 128
MAGIC = 12582912.0
BIG = 1.0e6


class Sizes:

    def __init__(self, n, d, e, experts, f):
        self.N, self.D, self.EDGES, self.E, self.F = n, d, e, experts, f
        self.CH = -(-n // P)
        self.FULL = n // P
        self.REST = n - self.FULL * P
        self.T = -(-e // P)
        self.TG = -(-self.T // P)
        self.CW = P // self.CH
        self.W = -(-n // self.CW)
        self.M = self.CW * self.CH
        self.BATCH = 16
        steps = self.T + self.W - 1
        self.NB = -(-steps // self.BATCH)
        self.NB += self.NB % 2
        self.STEPS = self.NB * self.BATCH
        self.CA = 15
        self.CB = self.CH - self.CA
        self.LAYERS = 3
        self.TB = 2 * P
        self.MT = (2 * n + experts * (self.TB - 1)) // self.TB
        self.MT += self.MT % 2


def rows_of(x, s):
    return (x[0:s.FULL * P, :].rearrange("(c p) d -> p c d", p=P), x[s.FULL * P:s.N, :])


def rsqrt(v, link, out, root, value, fix):
    link(v.reciprocal(out, root))
    link(v.tensor_tensor(fix, out, out, ALU.mult))
    link(v.tensor_tensor(fix, fix, value, ALU.mult))
    link(v.tensor_scalar(fix, fix, -0.5, 1.5, ALU.mult, ALU.add))


def phase_tables(nc, s, x, src, dst, ew, hf, tab):
    with ExitStack() as ctx:
        def sb(name, shape, dt=F32):
            return ctx.enter_context(nc.sbuf_tensor(name, shape, dt))

        def sem(name):
            return ctx.enter_context(nc.semaphore(name))

        TG, ST, M, CW, CH = s.TG, s.STEPS, s.M, s.CW, s.CH
        H2 = ST // 2
        src_i = sb("src_i", [P, TG, P], I32)
        dst_i = sb("dst_i", [P, TG, P], I32)
        val = sb("val", [P, TG, P])
        hi_i = sb("hi_i", [P, TG, P], I32)
        lo_i = sb("lo_i", [P, TG, P], I32)
        dst_f = sb("dst_f", [P, TG, P])
        hi_f = sb("hi_f", [P, TG, P])
        key_f = sb("key_f", [P, TG, P])
        rest1 = sb("rest1", [P, TG, P])
        rest2 = sb("rest2", [P, TG, P])
        parts = sb("parts", [P, 7, TG, P], BF16)
        tile_id = sb("tile_id", [P, TG])
        last_w = sb("last_w", [P, TG])
        far = sb("far", [P, TG])
        end_step = sb("end_step", [P, TG])
        step_id = sb("step_id", [P, ST])
        passed = sb("passed", [P, TG, ST], BF16)
        onehot_t = sb("onehot_t", [P, TG, ST], BF16)
        ones = sb("ones", [P, P], BF16)
        tile_of = sb("tile_of", [P, ST])
        win_of = sb("win_of", [P, ST])
        rel = sb("rel", [P, ST])
        col_w = sb("col_w", [P, CH * P])
        ended = sb("ended", [P, TG, CH * P], BF16)
        node_id = sb("node_id", [P, CH])
        idx_f = sb("idx_f", [P, CH])
        stats = sb("stats", [P, CH, 6])
        mv = sb("mv", [P, CH, 2])
        std = sb("std", [P, CH])
        fix = sb("fix", [P, CH])
        rstd = sb("rstd", [P, CH])
        shift = sb("shift", [P, CH])
        ps_t = ctx.enter_context(nc.psum_tensor("ps_t", [P, ST], F32))
        ps_e = ctx.enter_context(nc.psum_tensor("ps_e", [P, 6, H2], F32))

        cleared = sem("cleared")
        edges_in = sem("edges_in")
        x_in = sem("x_in")
        iotas = sem("iotas")
        link_dve = sem("link_dve")
        link_pool = sem("link_pool")
        last_ready = sem("last_ready")
        passed_ready = sem("passed_ready")
        tiles_counted = sem("tiles_counted")
        hot_ready = sem("hot_ready")
        parts_ready = sem("parts_ready")
        expanded = sem("expanded")
        copied = sem("copied")
        ended_ready = sem("ended_ready")
        ended_counted = sem("ended_counted")
        stats_ready = sem("stats_ready")
        mv_ready = sem("mv_ready")
        std_ready = sem("std_ready")
        rstd_ready = sem("rstd_ready")

        block = ctx.enter_context(nc.Block())
        head = (TG - 1) * P * P
        rows = s.EDGES // P - (TG - 1) * P
        rest = s.EDGES % P

        @block.sync
        def _(sp):
            for dram, tile in ((dst, dst_i), (src, src_i), (ew, val)):
                sp.dma_start(tile[:, 0:TG - 1, :],
                             dram[0:head].rearrange("(g p e) -> p g e", p=P, e=P)).then_inc(edges_in, 16)
            sp.wait_ge(cleared, 3)
            for dram, tile in ((dst, dst_i), (src, src_i), (ew, val)):
                sp.dma_start(tile[0:rows, TG - 1, :],
                             dram[head:head + rows * P].rearrange("(p e) -> p e", e=P)).then_inc(edges_in, 16)
                sp.dma_start(tile[rows:rows + 1, TG - 1, 0:rest],
                             dram[head + rows * P:s.EDGES].rearrange("(p e) -> p e", p=1)).then_inc(edges_in, 16)
            full, tail = rows_of(x, s)
            sp.dma_start(hf[:, 0:s.FULL, :], full).then_inc(x_in, 16)
            sp.wait_ge(cleared, 4)
            sp.dma_start(hf[0:s.REST, s.FULL, :], tail).then_inc(x_in, 16)

        @block.gpsimd
        def _(pool):
            g = nc.gpsimd
            kw = dict(allow_small_or_imprecise_dtypes=True)
            for t in (dst_i, src_i, val, hf):
                g.memset(t[:, t.shape[1] - 1, :], 0).then_inc(cleared, 1)
            g.iota(tile_id[:], pattern=[[P, TG]], base=0, channel_multiplier=1, **kw).then_inc(iotas, 1)
            g.iota(step_id[:], pattern=[[1, ST]], base=0, channel_multiplier=0, **kw).then_inc(iotas, 1)
            g.memset(ones[:], 1.0).then_inc(iotas, 1)
            g.iota(node_id[:], pattern=[[P, CH]], base=0, channel_multiplier=1, **kw).then_inc(iotas, 1)
            g.iota(col_w[:], pattern=[[1, CH * P]], base=0, channel_multiplier=0, **kw).then_inc(link_pool, 1)
            pool.wait_ge(link_pool, 1)
            g.tensor_scalar(col_w[:], col_w[:], 1.0 / CW, -(CW - 1) / 2.0 / CW, ALU.mult, ALU.add).then_inc(link_pool, 1)
            pool.wait_ge(link_pool, 2)
            g.tensor_scalar(col_w[:], col_w[:], MAGIC, None, ALU.add).then_inc(link_pool, 1)
            pool.wait_ge(link_pool, 3)
            g.tensor_scalar(col_w[:], col_w[:], -MAGIC, None, ALU.add).then_inc(link_pool, 1)
            pool.wait_ge(link_pool, 4)
            pool.wait_ge(rstd_ready, 2)
            pool.wait_ge(x_in, 32)
            for c in range(CH):
                g.tensor_scalar(hf[:, c, :], hf[:, c, :], rstd[:, c:c + 1], shift[:, c:c + 1], ALU.mult, ALU.add)

        @block.scalar
        def _(act):
            a = nc.scalar
            act.wait_ge(mv_ready, 1)
            a.activation(std[:], mv[:, :, 1], ACT.Sqrt).then_inc(std_ready, 1)

        @block.vector
        def _(dve):
            v = nc.vector
            count = [0]

            def link(ins):
                count[0] += 1
                ins.then_inc(link_dve, 1)
                dve.wait_ge(link_dve, count[0])

            dve.wait_ge(iotas, 4)
            dve.wait_ge(edges_in, 16 * 9)
            link(v.tensor_copy(dst_f[:], dst_i[:]))
            link(v.tensor_reduce(last_w[:], dst_f[:], AX.X, ALU.max))
            link(v.tensor_scalar(last_w[:], last_w[:], 1.0 / CW, -(CW - 1) / 2.0 / CW, ALU.mult, ALU.add))
            link(v.tensor_scalar(last_w[:], last_w[:], MAGIC, None, ALU.add))
            link(v.tensor_scalar(last_w[:], last_w[:], -MAGIC, None, ALU.add))
            link(v.tensor_scalar(far[:], tile_id[:], float(s.T - 1) - 0.5, BIG, ALU.is_gt, ALU.mult))
            link(v.tensor_tensor(last_w[:], last_w[:], far[:], ALU.add))
            v.tensor_tensor(end_step[:], last_w[:], tile_id[:], ALU.add).then_inc(last_ready, 1)
            dve.wait_ge(last_ready, 1)
            for k in range(TG):
                v.tensor_scalar(passed[:, k, :], step_id[:], end_step[:, k:k + 1], None,
                                ALU.is_gt).then_inc(passed_ready, 1)
            link(v.tensor_scalar(hi_i[:], src_i[:], 7, None, ALU.arith_shift_right))
            link(v.tensor_scalar(lo_i[:], src_i[:], 127, None, ALU.bitwise_and))
            link(v.tensor_copy(hi_f[:], hi_i[:]))
            link(v.tensor_copy(parts[:, 3, :, :], lo_i[:]))
            link(v.scalar_tensor_tensor(key_f[:], dst_f[:], float(CH), hi_f[:], ALU.mult, ALU.add))
            for k, f in ((0, key_f), (4, val)):
                link(v.tensor_copy(parts[:, k, :, :], f[:]))
                link(v.tensor_tensor(rest1[:], f[:], parts[:, k, :, :], ALU.subtract))
                link(v.tensor_copy(parts[:, k + 1, :, :], rest1[:]))
                link(v.tensor_tensor(rest2[:], rest1[:], parts[:, k + 1, :, :], ALU.subtract))
                v.tensor_copy(parts[:, k + 2, :, :], rest2[:]).then_inc(parts_ready, 1)
                dve.wait_ge(parts_ready, 1 + k // 4)
            dve.wait_ge(tiles_counted, 1)
            link(v.tensor_copy(tile_of[:], ps_t[:]))
            for k in range(TG):
                v.tensor_scalar(onehot_t[:, k, :], tile_of[:], tile_id[:, k:k + 1], None,
                                ALU.is_equal).then_inc(hot_ready, 1)
            link(v.tensor_tensor(win_of[:], step_id[:], tile_of[:], ALU.subtract))
            v.memset(tab.same[:, 0:1], 0.0)
            v.tensor_tensor(tab.same[:, 1:ST], tile_of[:, 1:ST], tile_of[:, 0:ST - 1], ALU.subtract)
            dve.wait_ge(x_in, 32)
            for c in range(CH):
                v.bn_stats(stats[:, c, :], hf[:, c, :]).then_inc(stats_ready, 1)
            for c in range(CH):
                dve.wait_ge(stats_ready, c + 1)
                ins = v.bn_aggr(mv[:, c, :], stats[:, c, :])
            link(ins)
            v.tensor_scalar(mv[:, :, 1], mv[:, :, 1], 1e-5, None, ALU.add).then_inc(mv_ready, 1)
            for k in range(2):
                half = slice(k * H2, (k + 1) * H2)
                dve.wait_ge(expanded, 1 + k)
                link(v.scalar_tensor_tensor(rel[:, half], win_of[:, half], -float(M), ps_e[:, k, :],
                                            ALU.mult, ALU.add))
            v.tensor_scalar(tab.key[:], rel[:], -1.0, float(M), ALU.max, ALU.min).then_inc(copied, 1)
            dests = [tab.lo, tab.w[0], tab.w[1], tab.w3]
            for q in range(4):
                for k in range(2):
                    dve.wait_ge(expanded, 3 + 2 * q + k)
                    v.tensor_copy(dests[q][:, k * H2:(k + 1) * H2], ps_e[:, (2 + 2 * q + k) % 6, :]).then_inc(copied, 1)
            dve.wait_ge(std_ready, 1)
            rsqrt(v, link, rstd[:], std[:], mv[:, :, 1], fix[:])
            rstd_done = v.tensor_tensor(rstd[:], rstd[:], fix[:], ALU.mult)
            rstd_done.then_inc(rstd_ready, 1)
            dve.wait_ge(rstd_ready, 1)
            v.scalar_tensor_tensor(shift[:], mv[:, :, 0], -1.0, rstd[:], ALU.mult, ALU.mult).then_inc(rstd_ready, 1)
            dve.wait_ge(link_pool, 4)
            for k in range(TG):
                v.tensor_scalar(ended[:, k, :], col_w[:], last_w[:, k:k + 1], None, ALU.is_ge).then_inc(ended_ready, 1)
            dve.wait_ge(ended_counted, 1)
            link(v.scalar_tensor_tensor(idx_f[:], ps_t[:, 0:CH], float(CW), node_id[:], ALU.mult, ALU.add))
            link(v.tensor_scalar(idx_f[:], idx_f[:], float(ST * CW - 1), None, ALU.min))
            link(v.tensor_copy(tab.gather[:], idx_f[:]))

        @block.tensor
        def _(pe):
            t = nc.tensor
            pe.wait_ge(passed_ready, TG)
            for k in range(2):
                for g in range(TG):
                    ins = t.matmul(ps_t[:, k * H2:(k + 1) * H2], ones[:, :], passed[:, g, k * H2:(k + 1) * H2],
                                   start=(g == 0), stop=(g == TG - 1))
            ins.then_inc(tiles_counted, 1)
            pe.wait_ge(hot_ready, TG)
            pe.wait_ge(parts_ready, 2)

            def expand(names, slot):
                for k in range(2):
                    for n, (q, g) in enumerate((q, g) for q in names for g in range(TG)):
                        ins = t.matmul(ps_e[:, slot + k, :], parts[:, q, g, :],
                                       onehot_t[:, g, k * H2:(k + 1) * H2], start=(n == 0),
                                       stop=(n == TG * len(names) - 1))
                    ins.then_inc(expanded, 1)

            expand((0, 1, 2), 0)
            expand((3,), 2)
            expand((4,), 4)
            pe.wait_ge(copied, 1)
            expand((5,), 0)
            pe.wait_ge(copied, 3)
            expand((6,), 2)
            pe.wait_ge(ended_ready, TG)
            pe.wait_ge(hot_ready, TG)
            for c in range(CH):
                for g in range(TG):
                    ins = t.matmul(ps_t[:, c:c + 1], ended[:, g, c * P:(c + 1) * P], ones[:, 0:1],
                                   start=(g == 0), stop=(g == TG - 1))
            ins.then_inc(ended_counted, 1)


def phase_build(nc, s, tab, a_dram, xs_dram, acc):
    with ExitStack() as ctx:
        def sb(name, shape, dt=F32):
            return ctx.enter_context(nc.sbuf_tensor(name, shape, dt))

        def sem(name):
            return ctx.enter_context(nc.semaphore(name))

        B, M, CW, CH, NB = s.BATCH, s.M, s.CW, s.CH, s.NB
        Q = B // 4
        lo_tab = sb("lo_tab", [P, P, B], BF16)
        key_tab = sb("key_tab", [P, M, B], BF16)
        lo_hot = sb("lo_hot", [P, 2, P, B], BF16)
        key_hot = sb("key_hot", [P, 2, M, B], BF16)
        key_w = sb("key_w", [P, 2, 3, M, B], BF16)
        w3_b = sb("w3_b", [P, 2, B])
        same_b = sb("same_b", [P, 2, B])
        win = sb("win", [P, 2, B, P])
        zeros = sb("zeros", [P, 4 * s.D])
        ps_w = ctx.enter_context(nc.psum_tensor("ps_w", [P, 2, B, P], F32))

        tabs = sem("tabs")
        xs_cleared = sem("xs_cleared")
        key_ready = sem("key_ready")
        hot_ready = sem("hot_ready")
        w3_read = sem("w3_read")
        third_ready = sem("third_ready")
        multiplied = sem("multiplied")
        same_ready = sem("same_ready")
        summed = sem("summed")
        stored = [sem(f"stored_{u}") for u in range(2)]

        block = ctx.enter_context(nc.Block())

        def at(b):
            return slice(b * B, (b + 1) * B) if isinstance(b, int) else bass.DynSlice(b * B, B)

        def late(b, first):
            return not isinstance(b, int) or b >= first

        @block.sync
        def _(sp):
            def store(b, u):
                sp.wait_ge(summed, (b + 1) * B)
                sp.dma_start(a_dram[0][at(b), :, :].rearrange("i p l -> p i l"),
                             win[0:CW * s.CA, u, :, :]).then_inc(stored[u], 16)

            sp.wait_ge(tabs, 5)
            flat = xs_dram.rearrange("(n p k) d -> n p (k d)", p=P, k=4)
            for n in range(s.MT * s.TB // (P * 4)):
                sp.dma_start(flat[n], zeros[:, :]).then_inc(xs_cleared, 16)
            with sp.Fori(0, NB // 2) as it:
                for u in range(2):
                    store(it * 2 + u, u)
            sp.wait_ge(xs_cleared, 16 * (s.MT * s.TB // (P * 4)))
            for u in range(2):
                sp.wait_ge(stored[u], 32 * (NB // 2))

        @block.gpsimd
        def _(pool):
            g = nc.gpsimd
            kw = dict(allow_small_or_imprecise_dtypes=True)
            g.iota(key_tab[:, 0:CW * s.CA, :], pattern=[[CH, CW], [1, s.CA], [0, B]], base=0,
                   channel_multiplier=0, **kw).then_inc(tabs, 1)
            g.iota(key_tab[:, CW * s.CA:M, :], pattern=[[CH, CW], [1, s.CB], [0, B]], base=s.CA,
                   channel_multiplier=0, **kw).then_inc(tabs, 1)
            g.iota(lo_tab[:], pattern=[[1, P], [0, B]], base=0, channel_multiplier=0, **kw).then_inc(tabs, 1)
            g.memset(win[:, 1, B - 1, :], 0.0).then_inc(tabs, 1)
            g.memset(zeros[:], 0.0).then_inc(tabs, 1)
            g.memset(acc[:], 0.0)

        @block.scalar
        def _(act):
            a = nc.scalar

            def third(b, u):
                if late(b, 2):
                    act.wait_ge(third_ready, (b - 1) * B)
                    act.wait_ge(multiplied, (b - 1) * Q)
                a.activation(w3_b[:, u, :], tab.w3[:, at(b)], ACT.Copy).then_inc(w3_read, 1)
                act.wait_ge(w3_read, b + 1)
                act.wait_ge(key_ready, b + 1)
                for j in range(B):
                    a.activation(key_w[:, u, 2, :, j], key_hot[:, u, :, j], ACT.Copy,
                                 scale=w3_b[:, u, j:j + 1]).then_inc(third_ready, 1)

            def store(b, u):
                act.wait_ge(summed, (b + 1) * B)
                act.dma_start(a_dram[1][at(b), :, :].rearrange("i p l -> p i l"),
                              win[CW * s.CA:M, u, :, :]).then_inc(stored[u], 16)

            third(0, 0)
            third(1, 1)
            store(0, 0)
            with act.Fori(1, NB // 2) as it:
                third(it * 2, 0)
                store(it * 2 - 1, 1)
                third(it * 2 + 1, 1)
                store(it * 2, 0)
            store(NB - 1, 1)

        @block.vector
        def _(dve):
            v = nc.vector

            def masks(b, u):
                if late(b, 2):
                    dve.wait_ge(multiplied, (b - 1) * Q)
                    dve.wait_ge(third_ready, (b - 1) * B)
                v.tensor_tensor(key_hot[:, u, :, :], key_tab[:, :, :],
                                tab.key[:, at(b)].unsqueeze(1).broadcast_to([P, M, B]),
                                ALU.is_equal).then_inc(key_ready, 1)
                v.tensor_tensor(lo_hot[:, u, :, :], lo_tab[:, :, :],
                                tab.lo[:, at(b)].unsqueeze(1).broadcast_to([P, P, B]),
                                ALU.is_equal).then_inc(hot_ready, 1)
                dve.wait_ge(key_ready, b + 1)
                for k in range(2):
                    v.tensor_tensor(key_w[:, u, k, :, :], key_hot[:, u, :, :],
                                    tab.w[k][:, at(b)].unsqueeze(1).broadcast_to([P, M, B]),
                                    ALU.mult).then_inc(hot_ready, 1)

            def sums(b, u):
                if late(b, 1):
                    dve.wait_ge(summed, b * B)
                v.tensor_copy(same_b[:, u, :], tab.same[:, at(b)]).then_inc(same_ready, 1)
                dve.wait_ge(same_ready, b + 1)
                if late(b, 2):
                    dve.wait_ge(stored[u], (b - u) * 16)
                for j in range(B):
                    if j % 4 == 0:
                        dve.wait_ge(multiplied, b * Q + (j // 4 + 1))
                    so_far = win[0:M, u, j - 1, :] if j else win[0:M, 1 - u, B - 1, :]
                    if late(b, 1) or j:
                        dve.wait_ge(summed, b * B + j)
                    v.scalar_tensor_tensor(win[0:M, u, j, :], so_far, same_b[0:M, u, j:j + 1],
                                           ps_w[0:M, u, j, :], ALU.mult, ALU.add).then_inc(summed, 1)

            dve.wait_ge(tabs, 4)
            masks(0, 0)
            masks(1, 1)
            sums(0, 0)
            masks(2, 0)
            sums(1, 1)
            masks(3, 1)
            sums(2, 0)
            with dve.Fori(2, NB // 2) as it:
                masks(it * 2, 0)
                sums(it * 2 - 1, 1)
                masks(it * 2 + 1, 1)
                sums(it * 2, 0)
            sums(NB - 1, 1)

        @block.tensor
        def _(pe):
            def multiply(b, u):
                pe.wait_ge(hot_ready, (b + 1) * 3)
                if late(b, 2):
                    pe.wait_ge(summed, (b - 1) * B)
                for j in range(B):
                    pe.wait_ge(third_ready, b * B + (j + 1))
                    for k in range(3):
                        ins = nc.tensor.matmul(ps_w[0:M, u, j, :], key_w[:, u, k, :, j], lo_hot[:, u, :, j],
                                               start=(k == 0), stop=(k == 2))
                    if j % 4 == 3:
                        ins.then_inc(multiplied, 1)

            multiply(0, 0)
            multiply(1, 1)
            with pe.Fori(1, NB // 2) as it:
                for u in range(2):
                    multiply(it * 2 + u, u)


def phase_rounds(nc, s, tab_gather, a_dram, acc, hf, x, x1):
    with ExitStack() as ctx:
        def sb(name, shape, dt=F32):
            return ctx.enter_context(nc.sbuf_tensor(name, shape, dt))

        def sem(name):
            return ctx.enter_context(nc.semaphore(name))

        CH, CA, CB, D = s.CH, s.CA, s.CB, s.D
        SPR = 2 * CH
        a_raw = sb("a_raw", [P, 2, CA * P])
        a_high = sb("a_high", [P, 2, CA * P], F32R)
        a_low = sb("a_low", [P, 2, CA * P], F32R)
        h_high = sb("h_high", [P, CH, D], F32R)
        h_low = sb("h_low", [P, CH, D], F32R)
        squares = sb("squares", [P, D])
        ssq = sb("ssq", [P, CH])
        root = sb("root", [P, CH])
        rinv = sb("rinv", [P, CH])
        fix = sb("fix_h", [P, CH])
        go_tile = sb("go_tile", [P, 1])
        ps = ctx.enter_context(nc.psum_tensor("ps_rows", [P, 16, D], F32))

        gathered = [sem(f"gathered_{u}") for u in range(2)]
        high_split = sem("high_split")
        low_split = sem("low_split")
        go = sem("gather_may_start")
        step_done = sem("step_done")
        h_high_ready = sem("h_high_ready")
        h_low_ready = sem("h_low_ready")
        acc_added = sem("acc_added")
        evac_act = sem("evac_act")
        evac_dve = sem("evac_dve")
        squared = sem("squared")
        clamped = sem("clamped")
        rooted = sem("rooted")
        link_dve = sem("link_norm")
        scaled = sem("scaled")
        x_in = sem("x_again_in")
        x1_cleared = sem("x1_cleared")
        LINKS = 10

        block = ctx.enter_context(nc.Block())
        chunks = [range(0, CA), range(CA, CH)]
        banks = [[(n // 2, r[n], min(2, len(r) - n)) for n in range(0, len(r), 2)] for r in chunks]
        even = [[b for b in bs if b[0] % 2 == 0] for bs in banks]
        odd = [[b for b in bs if b[0] % 2] for bs in banks]
        n_even, n_odd = sum(map(len, even)), sum(map(len, odd))
        width = [CA * P, CB * P]

        def pass_of(k):
            return (k % SPR) // CH

        @block.sync
        def _(sp):
            full, tail = rows_of(x, s)
            sp.dma_start(x1[:, 0:s.FULL, :], full).then_inc(x_in, 16)
            sp.wait_ge(x1_cleared, 1)
            sp.dma_start(x1[0:s.REST, s.FULL, :], tail).then_inc(x_in, 16)
            sp.wait_ge(x_in, 32)

        @block.gpsimd
        def _(pool):
            g = nc.gpsimd

            def gather(step, k):
                if not isinstance(step, int):
                    pool.wait_ge(low_split, step - 1)
                    pool.wait_ge(go, step - 1)
                    g.tensor_tensor(go_tile[:], go_tile[:], go_tile[:], ALU.add).then_inc(go, 1)
                which = pass_of(k)
                g.indirect_dma_start(
                    out=a_raw[:, k % 2, 0:width[which]], out_offset=None,
                    in_=a_dram[which].rearrange("i (c r) l -> (i c) (r l)", c=s.CW),
                    in_offset=bass.IndirectOffsetOnAxis(ap=tab_gather[:, k % CH:k % CH + 1], axis=0),
                ).then_inc(gathered[k % 2], 16)

            g.memset(go_tile[:], 0.0).then_inc(go, 1)
            gather(0, 0)
            gather(1, 1)
            g.memset(x1[:, s.FULL, :], 0.0).then_inc(x1_cleared, 1)
            with pool.Fori(0, s.LAYERS) as layer:
                for k in range(2, SPR + 2):
                    if k == 4:
                        for c in range(CH):
                            pool.wait_ge(scaled, layer * CH + (c + 1))
                            g.tensor_tensor(acc[:, c, :], acc[:, c, :], hf[:, c, :], ALU.add).then_inc(acc_added, 1)
                    gather(layer * SPR + k, k)
            for u in range(2):
                pool.wait_ge(gathered[u], 16 * (s.LAYERS * CH + 1))

        def splitter(eng, one):
            def run(layer, k0, k1):
                while k0 < k1 and (k0 % 2 or pass_of(k0) != pass_of(k0 + 1)):
                    one(layer * SPR + k0, k0)
                    k0 += 1
                pairs = (k1 - k0) // 2
                while pairs and pass_of(k0 + 2 * pairs - 1) != pass_of(k0):
                    pairs -= 1
                if pairs > 1:
                    with eng.Fori(0, pairs) as j:
                        one(layer * SPR + (j * 2 + k0), k0)
                        one(layer * SPR + (j * 2 + (k0 + 1)), k0 + 1)
                    k0 += 2 * pairs
                for k in range(k0, k1):
                    one(layer * SPR + k, k)
            return run

        @block.scalar
        def _(act):
            a = nc.scalar

            def high(step, k):
                u, n = k % 2, width[pass_of(k)]
                if isinstance(step, int):
                    act.wait_ge(gathered[u], 16)
                else:
                    act.wait_ge(gathered[u], (step - u) * 8 + 16)
                    act.wait_ge(step_done, step - 1)
                a.activation(a_high[:, u, 0:n], a_raw[:, u, 0:n], ACT.Copy).then_inc(high_split, 1)

            split = splitter(act, high)
            high(0, 0)
            high(1, 1)
            with act.Fori(0, s.LAYERS) as layer:
                for c in range(CH):
                    act.wait_ge(scaled, layer * CH + (c + 1))
                    a.activation(h_high[:, c, :], hf[:, c, :], ACT.Copy).then_inc(h_high_ready, 1)

                def evacuate(w):
                    act.wait_ge(step_done, layer * SPR + CH * (w + 1))
                    if w == 0:
                        act.wait_ge(h_low_ready, layer * CH + CH)
                        act.wait_ge(acc_added, layer * CH + CH)
                    for bank, c, n in even[w]:
                        a.activation(hf[:, c:c + n, :], ps[:, 2 * bank:2 * bank + n, :], ACT.Copy).then_inc(evac_act, 1)

                def square(w, cs):
                    act.wait_ge(evac_act, layer * n_even + sum(map(len, even[:w + 1])))
                    act.wait_ge(evac_dve, layer * n_odd + sum(map(len, odd[:w + 1])))
                    for c in cs:
                        if c:
                            act.wait_ge(squared, layer * CH + c)
                        else:
                            act.wait_ge(h_high_ready, layer * CH + CH)
                        a.activation(squares[:], hf[:, c, :], ACT.Square, accum_out=ssq[:, c:c + 1]).then_inc(squared, 1)

                def roots(w):
                    act.wait_ge(clamped, layer * 2 + (w + 1))
                    r = slice(chunks[w][0], chunks[w][-1] + 1)
                    a.activation(root[:, r], ssq[:, r], ACT.Sqrt).then_inc(rooted, 1)

                split(layer, 2, CH + 1)
                evacuate(0)
                for n in range(5):
                    split(layer, CH + 1 + n, CH + 2 + n)
                    square(0, range(3 * n, 3 * n + 3))
                roots(0)
                split(layer, CH + 6, SPR + 1)
                evacuate(1)
                split(layer, SPR + 1, SPR + 2)
                square(1, chunks[1])
                roots(1)

        @block.vector
        def _(dve):
            v = nc.vector
            dve.sem_inc(scaled, CH)

            def low(step, k):
                u, n = k % 2, width[pass_of(k)]
                dve.wait_ge(high_split, step + 1)
                v.tensor_tensor(a_low[:, u, 0:n], a_raw[:, u, 0:n], a_high[:, u, 0:n].bitcast(F32),
                                ALU.subtract).then_inc(low_split, 1)

            split = splitter(dve, low)
            low(0, 0)
            low(1, 1)
            with dve.Fori(0, s.LAYERS) as layer:
                for c in range(CH):
                    dve.wait_ge(h_high_ready, layer * CH + (c + 1))
                    v.tensor_tensor(h_low[:, c, :], hf[:, c, :], h_high[:, c, :].bitcast(F32),
                                    ALU.subtract).then_inc(h_low_ready, 1)

                def evacuate(w):
                    dve.wait_ge(step_done, layer * SPR + CH * (w + 1))
                    if w == 0:
                        dve.wait_ge(h_low_ready, layer * CH + CH)
                        dve.wait_ge(acc_added, layer * CH + CH)
                    for bank, c, n in odd[w]:
                        v.tensor_copy(hf[:, c:c + n, :], ps[:, 2 * bank:2 * bank + n, :]).then_inc(evac_dve, 1)

                def inverse(w):
                    r = slice(chunks[w][0], chunks[w][-1] + 1)
                    n = [w * LINKS // 2]

                    def link(ins):
                        n[0] += 1
                        ins.then_inc(link_dve, 1)
                        dve.wait_ge(link_dve, layer * LINKS + n[0])

                    dve.wait_ge(squared, layer * CH + chunks[w][-1] + 1)
                    v.tensor_scalar(ssq[:, r], ssq[:, r], 1e-24, None, ALU.max).then_inc(clamped, 1)
                    dve.wait_ge(rooted, layer * 2 + (w + 1))
                    rsqrt(v, link, rinv[:, r], root[:, r], ssq[:, r], fix[:, r])
                    link(v.tensor_tensor(rinv[:, r], rinv[:, r], fix[:, r], ALU.mult))

                def scale(cs):
                    for c in cs:
                        v.tensor_scalar(hf[:, c, :], hf[:, c, :], rinv[:, c:c + 1], None,
                                        ALU.mult).then_inc(scaled, 1)

                split(layer, 2, CH + 1)
                evacuate(0)
                split(layer, CH + 1, CH + 6)
                inverse(0)
                for n in range(5):
                    split(layer, CH + 6 + n, CH + 7 + n)
                    scale(range(3 * n, 3 * n + 3))
                split(layer, CH + 11, SPR + 1)
                evacuate(1)
                split(layer, SPR + 1, SPR + 2)
                inverse(1)
                scale(chunks[1])

        @block.tensor
        def _(pe):
            def step(n, k, c, first, last, layer):
                u, w = k % 2, pass_of(k)
                pe.wait_ge(low_split, n + 1)
                if w == 0:
                    pe.wait_ge(h_low_ready, layer * CH + (c + 1))
                for r in range(len(chunks[w])):
                    if first is not None and w == 1 and r % 2 == 0:
                        evac, per, nth = (evac_dve, n_odd, r // 4 + 1) if r // 2 % 2 else (evac_act, n_even, r // 4 + 1)
                        pe.wait_ge(evac, first * per + nth)
                    block_r = slice(r * P, (r + 1) * P)
                    for m, (a_part, h_part) in enumerate(((a_high, h_high), (a_high, h_low), (a_low, h_high))):
                        rhs = h_part[:, c, :] if isinstance(c, int) else \
                            h_part[:, bass.DynSlice(c, 1), :].rearrange("p c d -> p (c d)")
                        ins = nc.tensor.matmul(ps[:, r, :], a_part[:, u, block_r], rhs,
                                               start=(first is not None and m == 0 and r % 2 == 0), stop=(last and m == 2),
                                               skip_group_check=True)
                ins.then_inc(step_done, 1)

            with pe.Fori(0, s.LAYERS) as layer:
                for w in range(2):
                    k0 = w * CH
                    step(layer * SPR + k0, k0, 0, layer, False, layer)
                    with pe.Fori(0, (CH - 3) // 2) as j:
                        for t in (1, 2):
                            step(layer * SPR + (j * 2 + (k0 + t)), k0 + t, j * 2 + t, None, False, layer)
                    for c in (CH - 2, CH - 1):
                        step(layer * SPR + (k0 + c), k0 + c, c, None, c == CH - 1, layer)


def phase_route(nc, s, acc, hf, x1, y, gate_w, gate_b, b1, beta, routes, xs_dram):
    with ExitStack() as ctx:
        def sb(name, shape, dt=F32):
            return ctx.enter_context(nc.sbuf_tensor(name, shape, dt))

        def sem(name):
            return ctx.enter_context(nc.semaphore(name))

        CH, D, E, MT, F4 = s.CH, s.D, s.E, s.MT, s.F // P
        K2 = 2 * CH
        KD = D // P
        stats = sb("stats_y", [P, CH, 6])
        mv = sb("mv_y", [P, CH, 2])
        std = sb("std_y", [P, CH])
        rstd = sb("rstd_y", [P, CH])
        fix = sb("fix_y", [P, CH])
        shift = sb("shift_y", [P, CH])
        ident = sb("ident", [P, P])
        yT = sb("yT", [P, 4, KD, P])
        gw = sb("gw", [P, KD, E])
        gb = sb("gb", [P, E])
        bt = sb("bt", [P, D])
        b1_sb = sb("b1_sb", [E, s.F])
        logits = sb("logits", [P, CH, E])
        top = sb("top", [P, CH, 8])
        top_i = sb("top_i", [P, CH, 8], U32)
        gap = sb("gap", [P, CH])
        ex = sb("ex", [P, CH])
        den = sb("den", [P, CH])
        choice = sb("choice", [P, 2, CH])
        node_id = sb("node_id2", [P, CH])
        absent = sb("absent", [P, CH])
        e_row = sb("e_row", [P, E])
        e_part = sb("e_part", [P, 1])
        t_row = sb("t_row", [P, MT])
        all_ones = sb("all_ones", [P, E * K2])
        ones_b = sb("ones_b", [P, P], BF16)
        below = sb("below", [P, P], BF16)
        chosen = sb("chosen", [P, E, K2])
        running = sb("running", [P, E, K2])
        place = sb("place", [P, E, K2])
        count_f = sb("count_f", [P, E])
        count_b = sb("count_b", [P, E], BF16)
        prior = sb("prior", [P, E])
        n_tiles = sb("n_tiles", [P, E])
        tile_end = sb("tile_end", [P, E])
        base = sb("base", [P, E])
        pos_f = sb("pos_f", [P, K2])
        past = sb("past", [P, MT, E])
        expert_f = sb("expert_f", [P, MT])
        expert_hot = sb("expert_hot", [P, MT])
        ps_y = ctx.enter_context(nc.psum_tensor("ps_y", [P, 4, 4, P], F32))
        ps_l = ctx.enter_context(nc.psum_tensor("ps_l", [P, 512], F32))
        ps_c = ctx.enter_context(nc.psum_tensor("ps_c", [P, 512], F32))
        ps_b = ctx.enter_context(nc.psum_tensor("ps_b", [P, 512], F32))

        consts_in = sem("consts_in")
        tabs = sem("tabs_y")
        link_dve = sem("link_y")
        stats_ready = sem("stats_y_ready")
        mv_ready = sem("mv_y_ready")
        std_ready = sem("std_y_ready")
        shift_ready = sem("shift_ready")
        y_even = sem("y_even")
        y_odd = sem("y_odd")
        turned = sem("turned")
        turned_even = sem("turned_even")
        turned_odd = sem("turned_odd")
        gated = sem("gated")
        topped = sem("topped")
        exp_ready = sem("exp_ready")
        gap_ready = sem("gap_ready")
        counts = sem("counts")
        counted = sem("counted")
        placed = sem("placed")
        hot_ready = sem("expert_hot_ready")
        b1_ready = sem("b1_ready")
        sorted_out = sem("sorted_out")

        block = ctx.enter_context(nc.Block())

        @block.sync
        def _(sp):
            sp.dma_start(gw[:, :, :], gate_w.rearrange("(k p) e -> p k e", p=P)).then_inc(consts_in, 16)
            sp.dma_start(gb[:, :], gate_b.rearrange("(a e) -> a e", a=1).broadcast_to([P, E])).then_inc(consts_in, 16)
            sp.dma_start(bt[:, :], beta.rearrange("(a e) -> a e", a=1).broadcast_to([P, D])).then_inc(consts_in, 16)
            sp.dma_start(b1_sb[:, :], b1).then_inc(consts_in, 16)

        @block.gpsimd
        def _(pool):
            g = nc.gpsimd
            kw = dict(allow_small_or_imprecise_dtypes=True)
            g.memset(all_ones[:], 1.0).then_inc(tabs, 1)
            g.memset(ones_b[:], 1.0).then_inc(tabs, 1)
            pool.wait_ge(tabs, 2)
            g.affine_select(out=ident[:], in_=all_ones[:, 0:P], pattern=[[1, P]], compare_op=ALU.is_equal,
                            fill=0.0, base=0, channel_multiplier=-1).then_inc(tabs, 1)
            g.affine_select(out=below[:], in_=ones_b[:], pattern=[[1, P]], compare_op=ALU.is_gt,
                            fill=0.0, base=0, channel_multiplier=-1).then_inc(tabs, 1)
            g.iota(node_id[:], pattern=[[P, CH]], base=0, channel_multiplier=1, **kw).then_inc(tabs, 1)
            g.iota(e_row[:], pattern=[[1, E]], base=0, channel_multiplier=0, **kw).then_inc(tabs, 1)
            g.iota(e_part[:], pattern=[[0, 1]], base=0, channel_multiplier=1, **kw).then_inc(tabs, 1)
            g.iota(t_row[:], pattern=[[1, MT]], base=0, channel_multiplier=0, **kw).then_inc(tabs, 1)
            pool.wait_ge(placed, 1)
            for k in range(2):
                for c in range(CH):
                    n = P if c < s.FULL else s.REST
                    g.indirect_dma_start(
                        out=xs_dram, out_offset=bass.IndirectOffsetOnAxis(
                            ap=routes.place[0:n, k * CH + c:k * CH + c + 1], axis=0),
                        in_=y[0:n, c, :], in_offset=None).then_inc(sorted_out, 16)
            pool.wait_ge(consts_in, 64)
            for c in range(CH):
                g.tensor_tensor(x1[:, c, :], x1[:, c, :], bt[:], ALU.add)
            pool.wait_ge(sorted_out, 16 * K2)

        @block.scalar
        def _(act):
            a = nc.scalar
            act.wait_ge(mv_ready, 1)
            a.activation(std[:], mv[:, :, 1], ACT.Sqrt).then_inc(std_ready, 1)
            act.wait_ge(shift_ready, 1)
            for c in range(0, CH, 2):
                a.activation(y[:, c, :], x1[:, c, :], ACT.Identity, bias=shift[:, c:c + 1],
                             scale=rstd[:, c:c + 1]).then_inc(y_even, 1)
            for c in range(0, CH, 2):
                act.wait_ge(turned, c + 1)
                if c >= 4:
                    act.wait_ge(gated, c - 3)
                a.activation(yT[:, c % 4, :, :], ps_y[:, c % 4, 0:KD, :], ACT.Copy).then_inc(turned_even, 1)
            act.wait_ge(gap_ready, 1)
            a.activation(ex[:], gap[:], ACT.Exp).then_inc(exp_ready, 1)
            act.wait_ge(b1_ready, 1)
            a.activation(routes.b1[:].rearrange("p t f -> p f t"),
                         ps_b[:, 0:F4 * MT].rearrange("p (f t) -> p f t", t=MT), ACT.Copy)

        @block.vector
        def _(dve):
            v = nc.vector
            n_link = [0]

            def link(ins):
                n_link[0] += 1
                ins.then_inc(link_dve, 1)
                dve.wait_ge(link_dve, n_link[0])

            for c in range(CH):
                v.tensor_tensor(acc[:, c, :], acc[:, c, :], hf[:, c, :], ALU.add).then_inc(stats_ready, 1)
            for c in range(CH):
                dve.wait_ge(stats_ready, c + 1)
                v.scalar_tensor_tensor(x1[:, c, :], acc[:, c, :], 1.0 / (s.LAYERS + 1), x1[:, c, :],
                                       ALU.mult, ALU.add).then_inc(stats_ready, 1)
            for c in range(CH):
                dve.wait_ge(stats_ready, CH + c + 1)
                v.bn_stats(stats[:, c, :], x1[:, c, :]).then_inc(stats_ready, 1)
            for c in range(CH):
                dve.wait_ge(stats_ready, 2 * CH + c + 1)
                ins = v.bn_aggr(mv[:, c, :], stats[:, c, :])
            link(ins)
            v.tensor_scalar(mv[:, :, 1], mv[:, :, 1], 1e-5, None, ALU.add).then_inc(mv_ready, 1)
            dve.wait_ge(mv_ready, 1)
            dve.wait_ge(std_ready, 1)
            rsqrt(v, link, rstd[:], std[:], mv[:, :, 1], fix[:])
            link(v.tensor_tensor(rstd[:], rstd[:], fix[:], ALU.mult))
            v.scalar_tensor_tensor(shift[:], mv[:, :, 0], -1.0, rstd[:], ALU.mult, ALU.mult).then_inc(shift_ready, 1)
            dve.wait_ge(shift_ready, 1)
            for c in range(1, CH, 2):
                v.tensor_scalar(y[:, c, :], x1[:, c, :], rstd[:, c:c + 1], shift[:, c:c + 1],
                                ALU.mult, ALU.add).then_inc(y_odd, 1)
            for c in range(1, CH, 2):
                dve.wait_ge(turned, c + 1)
                if c >= 4:
                    dve.wait_ge(gated, c - 3)
                v.tensor_copy(yT[:, c % 4, :, :], ps_y[:, c % 4, 0:KD, :]).then_inc(turned_odd, 1)
            dve.wait_ge(consts_in, 64)
            dve.wait_ge(gated, CH)
            link(v.tensor_tensor(logits[:], ps_l[:, 0:CH * E].rearrange("p (c e) -> p c e", e=E),
                                 gb[:].unsqueeze(1).broadcast_to([P, CH, E]), ALU.add))
            for c in range(CH):
                v.max(top[:, c, :], logits[:, c, :]).then_inc(topped, 1)
            for c in range(CH):
                dve.wait_ge(topped, c + 1)
                ins = v.max_index(top_i[:, c, :], top[:, c, :], logits[:, c, :])
            link(ins)
            v.tensor_tensor(gap[:], top[:, :, 1], top[:, :, 0], ALU.subtract).then_inc(gap_ready, 1)
            dve.wait_ge(tabs, 8)
            link(v.tensor_scalar(absent[:], node_id[:], float(s.N) - 0.5, 100.0, ALU.is_gt, ALU.mult))
            for k in range(2):
                link(v.tensor_copy(choice[:, k, :], top_i[:, :, k]))
                link(v.tensor_tensor(choice[:, k, :], choice[:, k, :], absent[:], ALU.add))
            link(v.tensor_tensor(chosen[:], choice[:].rearrange("p k c -> p (k c)").unsqueeze(1).broadcast_to([P, E, K2]),
                                 e_row[:].unsqueeze(2).broadcast_to([P, E, K2]), ALU.is_equal))
            flat = chosen[:].rearrange("p e j -> p (e j)")
            link(v.tensor_tensor_scan(running[:].rearrange("p e j -> p (e j)"), all_ones[:], flat, 0.0,
                                      ALU.mult, ALU.add))
            link(v.memset(prior[:, 0:1], 0.0))
            link(v.tensor_copy(prior[:, 1:E], running[:, 0:E - 1, K2 - 1]))
            link(v.tensor_tensor(count_f[:], running[:, :, K2 - 1], prior[:], ALU.subtract))
            v.tensor_copy(count_b[:], count_f[:]).then_inc(counts, 1)
            dve.wait_ge(exp_ready, 1)
            link(v.tensor_scalar(den[:], ex[:], 1.0, None, ALU.add))
            link(v.reciprocal(routes.weight[:, 0, :], den[:]))
            link(v.tensor_tensor(routes.weight[:, 1, :], ex[:], routes.weight[:, 0, :], ALU.mult))
            dve.wait_ge(counted, 1)
            link(v.tensor_scalar(n_tiles[:], ps_c[:, 0:E], 1.0 / s.TB, (s.TB - 1) / 2.0 / s.TB, ALU.mult, ALU.add))
            link(v.tensor_scalar(n_tiles[:], n_tiles[:], MAGIC, None, ALU.add))
            link(v.tensor_scalar(n_tiles[:], n_tiles[:], -MAGIC, None, ALU.add))
            link(v.tensor_tensor_scan(tile_end[:], all_ones[:, 0:E], n_tiles[:], 0.0, ALU.mult, ALU.add))
            link(v.tensor_tensor(base[:], tile_end[:], n_tiles[:], ALU.subtract))
            link(v.scalar_tensor_tensor(base[:], base[:], float(s.TB), ps_c[:, E:2 * E], ALU.mult, ALU.add))
            link(v.scalar_tensor_tensor(base[:], base[:], -1.0, prior[:], ALU.add, ALU.subtract))
            link(v.tensor_tensor(place[:], running[:], base[:].unsqueeze(2).broadcast_to([P, E, K2]), ALU.add))
            link(v.tensor_tensor(place[:], place[:], chosen[:], ALU.mult))
            link(v.tensor_reduce(pos_f[:], place[:].rearrange("p e j -> p j e"), AX.X, ALU.add))
            v.tensor_copy(routes.place[:], pos_f[:]).then_inc(placed, 1)
            link(v.tensor_tensor(past[:], t_row[:].unsqueeze(2).broadcast_to([P, MT, E]),
                                 tile_end[:].unsqueeze(1).broadcast_to([P, MT, E]), ALU.is_ge))
            link(v.tensor_reduce(expert_f[:], past[:], AX.X, ALU.add))
            link(v.tensor_scalar(expert_f[:], expert_f[:], float(E - 1), None, ALU.min))
            link(v.tensor_copy(routes.expert[:], expert_f[:]))
            v.tensor_scalar(expert_hot[:], expert_f[:], e_part[:], None, ALU.is_equal).then_inc(hot_ready, 1)

        @block.tensor
        def _(pe):
            t = nc.tensor
            pe.wait_ge(tabs, 4)
            pe.wait_ge(consts_in, 64)

            def gate(c):
                pe.wait_ge((turned_odd if c % 2 else turned_even), c // 2 + 1)
                for k in range(KD):
                    ins = t.matmul(ps_l[:, c * E:(c + 1) * E], yT[:, c % 4, k, :], gw[:, k, :],
                                   start=(k == 0), stop=(k == KD - 1))
                ins.then_inc(gated, 1)

            for c in range(CH):
                pe.wait_ge((y_odd if c % 2 else y_even), c // 2 + 1)
                if c >= 4:
                    pe.wait_ge((turned_odd if c % 2 else turned_even), (c - 4) // 2 + 1)
                for k in range(KD):
                    ins = t.transpose(ps_y[:, c % 4, k, :], y[:, c, k * P:(k + 1) * P], ident[:, :])
                ins.then_inc(turned, 1)
                if c >= 2:
                    gate(c - 2)
            gate(CH - 2)
            gate(CH - 1)
            pe.wait_ge(counts, 1)
            t.matmul(ps_c[:, 0:E], ones_b[:, :], count_b[:, :], start=True, stop=True)
            t.matmul(ps_c[:, E:2 * E], below[:, :], count_b[:, :], start=True, stop=True).then_inc(counted, 1)
            pe.wait_ge(hot_ready, 1)
            for f in range(F4):
                ins = t.matmul(ps_b[:, f * MT:(f + 1) * MT], b1_sb[:, f * P:(f + 1) * P], expert_hot[0:E, :],
                               start=True, stop=True)
            ins.then_inc(b1_ready, 1)


class Routes:

    def __init__(self, nc, ctx, s):
        def sb(name, shape, dt=F32):
            return ctx.enter_context(nc.sbuf_tensor(name, shape, dt))

        self.place = sb("r_place", [P, 2 * s.CH], U32)
        self.weight = sb("r_weight", [P, 2, s.CH])
        self.expert = sb("r_expert", [P, s.MT], I32)
        self.b1 = sb("r_b1", [P, s.MT, s.F // P])


def phase_experts(nc, s, routes, w1, w2, b2, xs_dram, ys_dram):
    with ExitStack() as ctx:
        def sb(name, shape, dt=F32):
            return ctx.enter_context(nc.sbuf_tensor(name, shape, dt))

        def sem(name):
            return ctx.enter_context(nc.semaphore(name))

        D, F, MT, TB = s.D, s.F, s.MT, s.TB
        KD, KF, HALVES = D // P, F // P, TB // P
        WN = KD * F
        w_raw = [sb(f"w{n}_raw", [P, 2, WN]) for n in (1, 2)]
        w_high = [sb(f"w{n}_high", [P, 2, WN], F32R) for n in (1, 2)]
        w_low = [sb(f"w{n}_low", [P, 2, WN], F32R) for n in (1, 2)]
        b2_t = sb("b2_t", [P, 2, D])
        x_t = sb("x_t", [P, 2, HALVES, D])
        x_high = sb("x_high", [P, 2, KD, TB], F32R)
        x_low = sb("x_low", [P, 2, KD, TB], F32R)
        b1_t = sb("b1_t", [P, 2, KF])
        hid = sb("hid", [P, 2, KF, TB])
        hid_high = sb("hid_high", [P, 2, KF, TB], F32R)
        hid_low = sb("hid_low", [P, 2, KF, TB], F32R)
        y_t = sb("y_t", [P, 2, HALVES, D])
        ones = sb("ones_e", [P, P])
        ident = sb("ident_e", [P, P])
        ps_x = ctx.enter_context(nc.psum_tensor("ps_x", [P, 2, KD, TB], F32))
        ps_h = ctx.enter_context(nc.psum_tensor("ps_h", [P, 2, KF, TB], F32))
        ps_o = ctx.enter_context(nc.psum_tensor("ps_o", [P, 2, HALVES, D], F32))

        w_loaded = [[sem(f"w{n}_in_{u}") for u in range(2)] for n in (1, 2)]
        b2_loaded = [sem(f"b2_in_{u}") for u in range(2)]
        x_loaded = [sem(f"tokens_in_{u}") for u in range(2)]
        y_stored = [sem(f"results_out_{u}") for u in range(2)]
        tabs = sem("ident_ready")
        w_high_ready = [sem(f"w{n}_high_ready") for n in (1, 2)]
        w_low_ready = [sem(f"w{n}_low_ready") for n in (1, 2)]
        x_turned = sem("x_turned")
        x_high_ready = sem("x_high_ready")
        x_low_ready = sem("x_low_ready")
        first_done = sem("first_done")
        b1_ready = sem("b1_t_ready")
        hid_ready = sem("hid_ready")
        hid_high_ready = sem("hid_high_ready")
        hid_low_ready = sem("hid_low_ready")
        second_done = sem("second_done")
        y_ready = sem("y_ready")

        block = ctx.enter_context(nc.Block())

        def late(t, first):
            return not isinstance(t, int) or t >= first

        def one(t):
            return slice(t, t + 1) if isinstance(t, int) else bass.DynSlice(t, 1)

        def rows(t):
            return slice(t * TB, (t + 1) * TB) if isinstance(t, int) else bass.DynSlice(t * TB, TB)

        def nth(t, u):
            return (t - u) * 8 + 16

        def iterations(eng, last, run):
            for t in range(4):
                run(t, t % 2)
            pairs = (last + 1 - 4) // 2
            with eng.Fori(0, pairs) as j:
                run(j * 2 + 4, 0)
                run(j * 2 + 5, 1)
            for t in range(4 + 2 * pairs, last + 1):
                run(t, t % 2)

        def there(t):
            return not isinstance(t, int) or 0 <= t < MT

        @block.sync
        def _(sp):
            def expert_of(t):
                return sp.value_load(routes.expert[0:1, one(t)], min_val=0, max_val=s.E - 1)

            def weights(n, dram, t, u):
                e = expert_of(t)
                if late(t, 2):
                    sp.wait_ge(w_low_ready[n], t - 1)
                k = WN // dram.shape[2]
                sp.dma_start(w_raw[n][:, u, :].rearrange("p (k f) -> p k f", k=k),
                             dram[bass.DynSlice(e, 1), :, :].rearrange("a (k p) f -> p (a k) f", p=P),
                             ).then_inc(w_loaded[n][u], 16)

            def run(t, u):
                if there(t):
                    if late(t, 2):
                        sp.wait_ge(x_turned, t - 1)
                    sp.dma_start(x_t[:, u, :, :], xs_dram[rows(t), :].rearrange("(h p) d -> p h d", p=P),
                                 ).then_inc(x_loaded[u], 16)
                    weights(0, w1, t, u)
                if there(t - 1):
                    weights(1, w2, t - 1, 1 - u)
                if there(t - 2):
                    e = expert_of(t - 2)
                    if late(t - 2, 2):
                        sp.wait_ge(y_ready, (t - 3) * HALVES)
                    sp.dma_start(b2_t[:, u, :], b2[bass.DynSlice(e, 1), :].broadcast_to([P, D]),
                                 ).then_inc(b2_loaded[u], 16)

            for t in range(4):
                run(t, t % 2)
            with sp.Fori(2, MT // 2) as j:
                run(j * 2, 0)
                run(j * 2 + 1, 1)
            for t in (MT, MT + 1):
                run(t, t % 2)

        @block.gpsimd
        def _(pool):
            g = nc.gpsimd
            g.memset(ones[:], 1.0).then_inc(tabs, 1)
            pool.wait_ge(tabs, 1)
            g.affine_select(out=ident[:], in_=ones[:], pattern=[[1, P]], compare_op=ALU.is_equal,
                            fill=0.0, base=0, channel_multiplier=-1).then_inc(tabs, 1)

            def low(t, u):
                pool.wait_ge(hid_high_ready, t + 1)
                if late(t, 2):
                    pool.wait_ge(second_done, t - 1)
                g.tensor_tensor(hid_low[:, u, :, :], hid[:, u, :, :], hid_high[:, u, :, :].bitcast(F32),
                                ALU.subtract).then_inc(hid_low_ready, 1)

            for t in range(2):
                low(t, t)
            with pool.Fori(1, MT // 2) as j:
                low(j * 2, 0)
                low(j * 2 + 1, 1)

        @block.scalar
        def _(act):
            a = nc.scalar

            def weights(n, t, u):
                act.wait_ge(w_loaded[n][u], nth(t, u))
                if late(t, 2):
                    act.wait_ge((first_done, second_done)[n], t - 1)
                    act.wait_ge(w_low_ready[n], t - 1)
                a.activation(w_high[n][:, u, :], w_raw[n][:, u, :], ACT.Copy).then_inc(w_high_ready[n], 1)

            def tokens(t, u):
                act.wait_ge(x_turned, t + 1)
                if late(t, 2):
                    act.wait_ge(first_done, t - 1)
                a.activation(x_high[:, u, :, :], ps_x[:, u, :, :], ACT.Copy).then_inc(x_high_ready, 1)

            def hidden(t, u):
                if late(t, 2):
                    act.wait_ge(hid_ready, (t - 1) * KF)
                    act.wait_ge(hid_low_ready, t - 1)
                a.activation(b1_t[:, u, :], routes.b1[:, one(t), :].rearrange("p a f -> p (a f)"),
                             ACT.Copy).then_inc(b1_ready, 1)
                act.wait_ge(b1_ready, t + 1)
                act.wait_ge(first_done, t + 1)
                for f in range(KF):
                    a.activation(hid[:, u, f, :], ps_h[:, u, f, :], ACT.Relu,
                                 bias=b1_t[:, u, f:f + 1]).then_inc(hid_ready, 1)

            def store(t, u):
                act.wait_ge(y_ready, (t + 1) * HALVES)
                act.dma_start(ys_dram[rows(t), :].rearrange("(h p) d -> p h d", p=P),
                              y_t[:, u, :, :]).then_inc(y_stored[u], 16)

            def run(t, u):
                if there(t):
                    weights(1, t, u)
                if there(t + 1):
                    weights(0, t + 1, 1 - u)
                    tokens(t + 1, 1 - u)
                if there(t):
                    hidden(t, u)
                if there(t - 2):
                    store(t - 2, u)

            weights(0, 0, 0)
            tokens(0, 0)
            iterations(act, MT - 2, run)
            for t in (MT - 1, MT, MT + 1):
                run(t, t % 2)
            for u in range(2):
                act.wait_ge(y_stored[u], 16 * (MT // 2))

        @block.vector
        def _(dve):
            v = nc.vector

            def weights(n, t, u):
                dve.wait_ge(w_high_ready[n], t + 1)
                v.tensor_tensor(w_low[n][:, u, :], w_raw[n][:, u, :], w_high[n][:, u, :].bitcast(F32),
                                ALU.subtract).then_inc(w_low_ready[n], 1)

            def tokens(t, u):
                dve.wait_ge(x_high_ready, t + 1)
                v.tensor_tensor(x_low[:, u, :, :], ps_x[:, u, :, :], x_high[:, u, :, :].bitcast(F32),
                                ALU.subtract).then_inc(x_low_ready, 1)

            def hidden(t, u):
                dve.wait_ge(hid_ready, (t + 1) * KF)
                if late(t, 2):
                    dve.wait_ge(second_done, t - 1)
                    dve.wait_ge(hid_low_ready, t - 1)
                v.tensor_copy(hid_high[:, u, :, :], hid[:, u, :, :]).then_inc(hid_high_ready, 1)

            def result(t, u):
                dve.wait_ge(second_done, t + 1)
                if late(t, 2):
                    dve.wait_ge(y_stored[u], nth(t, u) - 16)
                dve.wait_ge(b2_loaded[u], nth(t, u))
                for h in range(HALVES):
                    v.tensor_tensor(y_t[:, u, h, :], ps_o[:, u, h, :], b2_t[:, u, :], ALU.add).then_inc(y_ready, 1)

            def run(t, u):
                if there(t):
                    weights(1, t, u)
                if there(t + 1):
                    weights(0, t + 1, 1 - u)
                    tokens(t + 1, 1 - u)
                if there(t):
                    hidden(t, u)
                if there(t - 1):
                    result(t - 1, 1 - u)

            weights(0, 0, 0)
            tokens(0, 0)
            iterations(dve, MT - 2, run)
            for t in (MT - 1, MT):
                run(t, t % 2)

        @block.tensor
        def _(pe):
            mm = nc.tensor.matmul

            def turn(t, u):
                pe.wait_ge(x_loaded[u], nth(t, u))
                if late(t, 2):
                    pe.wait_ge(x_low_ready, t - 1)
                for h in range(HALVES):
                    for k in range(KD):
                        ins = nc.tensor.transpose(ps_x[:, u, k, h * P:(h + 1) * P], x_t[:, u, h, k * P:(k + 1) * P],
                                                  ident[:, :])
                ins.then_inc(x_turned, 1)

            def first(t, u):
                pe.wait_ge(x_low_ready, t + 1)
                pe.wait_ge(w_low_ready[0], t + 1)
                if late(t, 2):
                    pe.wait_ge(hid_ready, (t - 1) * KF)
                for f in range(KF):
                    n = 0
                    for k in range(KD):
                        at = slice(k * F + f * P, k * F + (f + 1) * P)
                        for w, x in ((w_high, x_high), (w_high, x_low), (w_low, x_high)):
                            ins = mm(ps_h[:, u, f, :], w[0][:, u, at], x[:, u, k, :], start=(n == 0), stop=(n == 3 * KD - 1))
                            n += 1
                ins.then_inc(first_done, 1)

            def second(t, u):
                pe.wait_ge(hid_low_ready, t + 1)
                pe.wait_ge(w_low_ready[1], t + 1)
                if late(t, 2):
                    pe.wait_ge(y_ready, (t - 1) * HALVES)
                for half in range(HALVES):
                    n = 0
                    tokens = slice(half * P, (half + 1) * P)
                    for f in range(KF):
                        at = slice(f * D, (f + 1) * D)
                        for h, w in ((hid_high, w_high), (hid_high, w_low), (hid_low, w_high)):
                            ins = mm(ps_o[:, u, half, :], h[:, u, f, tokens], w[1][:, u, at],
                                     start=(n == 0), stop=(n == 3 * KF - 1))
                            n += 1
                ins.then_inc(second_done, 1)

            def run(t, u):
                if there(t + 1):
                    turn(t + 1, 1 - u)
                if there(t):
                    first(t, u)
                if there(t - 1):
                    second(t - 1, 1 - u)

            pe.wait_ge(tabs, 2)
            turn(0, 0)
            iterations(pe, MT - 2, run)
            for t in (MT - 1, MT):
                run(t, t % 2)


def phase_combine(nc, s, routes, x1, y, gamma, ys_dram, out):
    with ExitStack() as ctx:
        def sb(name, shape, dt=F32):
            return ctx.enter_context(nc.sbuf_tensor(name, shape, dt))

        def sem(name):
            return ctx.enter_context(nc.semaphore(name))

        CH, D = s.CH, s.D
        G = 5
        NG = CH // G
        found = sb("found", [P, CH, 2, D])
        gm = sb("gm", [P, D])
        stats = sb("stats_z", [P, CH, 6])
        mv = sb("mv_z", [P, CH, 2])
        std = sb("std_z", [P, CH])
        rstd = sb("rstd_z", [P, CH])
        fix = sb("fix_z", [P, CH])

        gm_in = sem("gm_in")
        found_in = [[sem(f"found_{g}_{k}") for k in range(2)] for g in range(NG)]
        mixed = sem("mixed")
        stats_ready = sem("stats_z_ready")
        mv_ready = sem("mv_z_ready")
        std_ready = sem("std_z_ready")
        link_dve = sem("link_z")
        scaled = sem("scaled_z")
        done = sem("rows_done")
        stored = sem("rows_stored")

        block = ctx.enter_context(nc.Block())

        def rows(c):
            return P if c < s.FULL else s.REST

        @block.sync
        def _(sp):
            sp.dma_start(gm[:, :], gamma.rearrange("(a e) -> a e", a=1).broadcast_to([P, D])).then_inc(gm_in, 16)
            for c in range(CH):
                sp.wait_ge(done, c + 1)
                sp.dma_start(out[c * P:c * P + rows(c), :], y[0:rows(c), c, :]).then_inc(stored, 16)
            sp.wait_ge(stored, 16 * CH)

        @block.gpsimd
        def _(pool):
            for c in range(CH):
                for k in range(2):
                    nc.gpsimd.indirect_dma_start(
                        out=found[0:rows(c), c, k, :], out_offset=None, in_=ys_dram,
                        in_offset=bass.IndirectOffsetOnAxis(
                            ap=routes.place[0:rows(c), k * CH + c:k * CH + c + 1], axis=0),
                    ).then_inc(found_in[c // G][k], 16)

        @block.scalar
        def _(act):
            for g in range(NG):
                act.wait_ge(mv_ready, g + 2)
                r = slice(g * G, (g + 1) * G)
                nc.scalar.activation(std[:, r], mv[:, r, 1], ACT.Sqrt).then_inc(std_ready, 1)

        @block.vector
        def _(dve):
            v = nc.vector
            n_link = [0]

            def link(ins):
                n_link[0] += 1
                ins.then_inc(link_dve, 1)
                dve.wait_ge(link_dve, n_link[0])

            v.memset(mv[:], 1.0).then_inc(mv_ready, 1)
            dve.wait_ge(mv_ready, 1)
            dve.wait_ge(gm_in, 16)
            n_mixed = 0
            for g in range(NG):
                cs = range(g * G, (g + 1) * G)
                r = slice(g * G, (g + 1) * G)
                for k in range(2):
                    dve.wait_ge(found_in[g][k], 16 * G)
                    for c in cs:
                        n = rows(c)
                        if k:
                            dve.wait_ge(mixed, n_mixed - G + 1)
                        v.scalar_tensor_tensor(y[0:n, c, :], found[0:n, c, k, :], routes.weight[0:n, k, c:c + 1],
                                               y[0:n, c, :], ALU.mult, ALU.add).then_inc(mixed, 1)
                        n_mixed += 1
                for c in cs:
                    dve.wait_ge(mixed, n_mixed - G + (c - g * G) + 1)
                    v.bn_stats(stats[0:rows(c), c, :], y[0:rows(c), c, :]).then_inc(stats_ready, 1)
                for c in cs:
                    dve.wait_ge(stats_ready, c + 1)
                    ins = v.bn_aggr(mv[0:rows(c), c, :], stats[0:rows(c), c, :])
                link(ins)
                v.tensor_scalar(mv[:, r, 1], mv[:, r, 1], 1e-5, None, ALU.add).then_inc(mv_ready, 1)
                dve.wait_ge(mv_ready, g + 2)
                dve.wait_ge(std_ready, g + 1)
                rsqrt(v, link, rstd[:, r], std[:, r], mv[:, r, 1], fix[:, r])
                link(v.tensor_tensor(rstd[:, r], rstd[:, r], fix[:, r], ALU.mult))
                for c in cs:
                    n = rows(c)
                    v.scalar_tensor_tensor(y[0:n, c, :], y[0:n, c, :], mv[0:n, c, 0:1], gm[0:n, :],
                                           ALU.subtract, ALU.mult).then_inc(scaled, 1)
                for c in cs:
                    n = rows(c)
                    dve.wait_ge(scaled, c + 1)
                    v.scalar_tensor_tensor(y[0:n, c, :], y[0:n, c, :], rstd[0:n, c:c + 1], x1[0:n, c, :],
                                           ALU.mult, ALU.add).then_inc(done, 1)


class Tables:

    def __init__(self, nc, ctx, s, gather):
        def sb(name, shape, dt=F32):
            return ctx.enter_context(nc.sbuf_tensor(name, shape, dt))

        self.gather = gather
        self.key = sb("tab_key", [P, s.STEPS], BF16)
        self.lo = sb("tab_lo", [P, s.STEPS], BF16)
        self.w = [sb(f"tab_w{k}", [P, s.STEPS], BF16) for k in (1, 2)]
        self.w3 = sb("tab_w3", [P, s.STEPS])
        self.same = sb("tab_same", [P, s.STEPS])


def program(nc, x, src, dst, edge_weight, gate_w, gate_b, w1, b1, w2, b2, gamma, beta, out):
    s = Sizes(x.shape[0], x.shape[1], src.shape[0], gate_w.shape[1], w1.shape[2])
    a_dram = [nc.dram_tensor(f"a_{i}", [s.STEPS, s.CW * n, P], F32, kind="Internal").ap()
              for i, n in enumerate((s.CA, s.CB))]
    xs_dram = nc.dram_tensor("tokens_sorted", [s.MT * s.TB, s.D], F32, kind="Internal").ap()
    ys_dram = nc.dram_tensor("results_sorted", [s.MT * s.TB, s.D], F32, kind="Internal").ap()
    with ExitStack() as ctx:
        def sb(name, shape, dt=F32):
            return ctx.enter_context(nc.sbuf_tensor(name, shape, dt))

        x1 = sb("x1", [P, s.CH, s.D])
        acc = sb("acc", [P, s.CH, s.D])
        routes = Routes(nc, ctx, s)
        gnn = ctx.enter_context(ExitStack())
        hf = gnn.enter_context(nc.sbuf_tensor("hf", [P, s.CH, s.D], F32))
        gather = gnn.enter_context(nc.sbuf_tensor("gather_rows", [P, s.CH], U32))
        with ExitStack() as stairs:
            tab = Tables(nc, stairs, s, gather)
            phase_tables(nc, s, x, src, dst, edge_weight, hf, tab)
            phase_build(nc, s, tab, a_dram, xs_dram, acc)
        phase_rounds(nc, s, gather, a_dram, acc, hf, x, x1)
        y = acc
        phase_route(nc, s, acc, hf, x1, y, gate_w, gate_b, b1, beta, routes, xs_dram)
        gnn.close()
        phase_experts(nc, s, routes, w1, w2, b2, xs_dram, ys_dram)
        phase_combine(nc, s, routes, x1, y, gamma, ys_dram, out)


NAMES = ["x", "src", "dst", "edge_weight", "L0_ffn_gate_w", "L0_ffn_gate_b", "L0_ffn_w1", "L0_ffn_b1",
         "L0_ffn_w2", "L0_ffn_b2", "L0_ffn_gamma", "L0_ffn_beta"]


def kernel(**inputs):
    import numpy as np
    import concourse.bacc as bacc
    from concourse.bass_utils import run_bass_kernel_spmd

    nc = bacc.Bacc("TRN2", target_bir_lowering=False, num_devices=1)
    arrays, aps = {}, []
    for name in NAMES:
        a = np.ascontiguousarray(inputs[name])
        arrays["in_" + name] = a
        aps.append(nc.dram_tensor("in_" + name, a.shape, mybir.dt.from_np(a.dtype), kind="ExternalInput").ap())
    out = nc.dram_tensor("out", inputs["x"].shape, F32, kind="ExternalOutput").ap()
    program(nc, *aps, out)
    result = run_bass_kernel_spmd(nc, [arrays], core_ids=[0])
    return result.results[0]["out"]
```

```python
from contextlib import ExitStack

import concourse.bass as bass
from concourse import mybir

F32 = mybir.dt.float32
F32R = mybir.dt.float32r
BF16 = mybir.dt.bfloat16
I32 = mybir.dt.int32
U32 = mybir.dt.uint32
ALU = mybir.AluOpType
ACT = mybir.ActivationFunctionType
AX = mybir.AxisListType

P = 128
MAGIC = 12582912.0
BIG = 1.0e6


class Sizes:

    def __init__(self, n, d, e, experts, f):
        self.N, self.D, self.EDGES, self.E, self.F = n, d, e, experts, f
        self.CH = -(-n // P)
        self.FULL = n // P
        self.REST = n - self.FULL * P
        self.T = -(-e // P)
        self.TG = -(-self.T // P)
        self.CW = P // self.CH
        self.W = -(-n // self.CW)
        self.M = self.CW * self.CH
        self.BATCH = 16
        steps = self.T + self.W - 1
        self.NB = -(-steps // self.BATCH)
        self.NB += self.NB % 2
        self.STEPS = self.NB * self.BATCH
        self.CA = 15
        self.CB = self.CH - self.CA
        self.LAYERS = 3
        self.TB = 2 * P
        self.MT = (2 * n + experts * (self.TB - 1)) // self.TB
        self.MT += self.MT % 2


def rows_of(x, s):
    return (x[0:s.FULL * P, :].rearrange("(c p) d -> p c d", p=P), x[s.FULL * P:s.N, :])


def rsqrt(v, link, out, root, value, fix):
    link(v.reciprocal(out, root))
    link(v.tensor_tensor(fix, out, out, ALU.mult))
    link(v.tensor_tensor(fix, fix, value, ALU.mult))
    link(v.tensor_scalar(fix, fix, -0.5, 1.5, ALU.mult, ALU.add))


def phase_tables(nc, s, x, src, dst, ew, hf, acc, tab):
    with ExitStack() as ctx:
        def sb(name, shape, dt=F32):
            return ctx.enter_context(nc.sbuf_tensor(name, shape, dt))

        def sem(name):
            return ctx.enter_context(nc.semaphore(name))

        TG, ST, M, CW, CH = s.TG, s.STEPS, s.M, s.CW, s.CH
        H2 = ST // 2
        src_i = sb("src_i", [P, TG, P], I32)
        dst_i = sb("dst_i", [P, TG, P], I32)
        val = sb("val", [P, TG, P])
        hi_i = sb("hi_i", [P, TG, P], I32)
        lo_i = sb("lo_i", [P, TG, P], I32)
        dst_f = sb("dst_f", [P, TG, P])
        hi_f = sb("hi_f", [P, TG, P])
        key_f = sb("key_f", [P, TG, P])
        rest1 = sb("rest1", [P, TG, P])
        rest2 = sb("rest2", [P, TG, P])
        parts = sb("parts", [P, 7, TG, P], BF16)
        tile_id = sb("tile_id", [P, TG])
        last_w = sb("last_w", [P, TG])
        far = sb("far", [P, TG])
        end_step = sb("end_step", [P, TG])
        step_id = sb("step_id", [P, ST])
        passed = sb("passed", [P, TG, ST], BF16)
        onehot_t = sb("onehot_t", [P, TG, ST], BF16)
        ones = sb("ones", [P, P], BF16)
        tile_of = sb("tile_of", [P, ST])
        win_of = sb("win_of", [P, ST])
        rel = sb("rel", [P, ST])
        col_w = sb("col_w", [P, CH * P])
        ended = sb("ended", [P, TG, CH * P], BF16)
        node_id = sb("node_id", [P, CH])
        idx_f = sb("idx_f", [P, CH])
        stats = sb("stats", [P, CH, 6])
        mv = sb("mv", [P, CH, 2])
        std = sb("std", [P, CH])
        fix = sb("fix", [P, CH])
        rstd = sb("rstd", [P, CH])
        shift = sb("shift", [P, CH])
        ps_t = ctx.enter_context(nc.psum_tensor("ps_t", [P, ST], F32))
        ps_e = ctx.enter_context(nc.psum_tensor("ps_e", [P, 6, H2], F32))

        cleared = sem("cleared")
        edges_in = sem("edges_in")
        x_in = sem("x_in")
        iotas = sem("iotas")
        link_dve = sem("link_dve")
        link_pool = sem("link_pool")
        last_ready = sem("last_ready")
        passed_ready = sem("passed_ready")
        tiles_counted = sem("tiles_counted")
        hot_ready = sem("hot_ready")
        parts_ready = sem("parts_ready")
        expanded = sem("expanded")
        copied = sem("copied")
        key_ready = sem("tab_key_ready")
        ended_ready = sem("ended_ready")
        ended_counted = sem("ended_counted")
        stats_ready = sem("stats_ready")
        mv_ready = sem("mv_ready")
        std_ready = sem("std_ready")
        rstd_ready = sem("rstd_ready")

        block = ctx.enter_context(nc.Block())
        head = (TG - 1) * P * P
        rows = s.EDGES // P - (TG - 1) * P
        rest = s.EDGES % P

        @block.sync
        def _(sp):
            for dram, tile in ((dst, dst_i), (src, src_i), (ew, val)):
                sp.dma_start(tile[:, 0:TG - 1, :],
                             dram[0:head].rearrange("(g p e) -> p g e", p=P, e=P)).then_inc(edges_in, 16)
            sp.wait_ge(cleared, 3)
            for dram, tile in ((dst, dst_i), (src, src_i), (ew, val)):
                sp.dma_start(tile[0:rows, TG - 1, :],
                             dram[head:head + rows * P].rearrange("(p e) -> p e", e=P)).then_inc(edges_in, 16)
                sp.dma_start(tile[rows:rows + 1, TG - 1, 0:rest],
                             dram[head + rows * P:s.EDGES].rearrange("(p e) -> p e", p=1)).then_inc(edges_in, 16)
            full, tail = rows_of(x, s)
            sp.dma_start(hf[:, 0:s.FULL, :], full).then_inc(x_in, 16)
            sp.wait_ge(cleared, 4)
            sp.dma_start(hf[0:s.REST, s.FULL, :], tail).then_inc(x_in, 16)

        @block.gpsimd
        def _(pool):
            g = nc.gpsimd
            kw = dict(allow_small_or_imprecise_dtypes=True)
            for t in (dst_i, src_i, val, hf):
                g.memset(t[:, t.shape[1] - 1, :], 0).then_inc(cleared, 1)
            g.iota(tile_id[:], pattern=[[P, TG]], base=0, channel_multiplier=1, **kw).then_inc(iotas, 1)
            g.iota(step_id[:], pattern=[[1, ST]], base=0, channel_multiplier=0, **kw).then_inc(iotas, 1)
            g.memset(ones[:], 1.0).then_inc(iotas, 1)
            g.iota(node_id[:], pattern=[[P, CH]], base=0, channel_multiplier=1, **kw).then_inc(iotas, 1)
            g.iota(col_w[:], pattern=[[1, CH * P]], base=0, channel_multiplier=0, **kw).then_inc(link_pool, 1)
            pool.wait_ge(link_pool, 1)
            g.tensor_scalar(col_w[:], col_w[:], 1.0 / CW, -(CW - 1) / 2.0 / CW,
                            ALU.mult, ALU.add).then_inc(link_pool, 1)
            pool.wait_ge(link_pool, 2)
            g.tensor_scalar(col_w[:], col_w[:], MAGIC, None, ALU.add).then_inc(link_pool, 1)
            pool.wait_ge(link_pool, 3)
            g.tensor_scalar(col_w[:], col_w[:], -MAGIC, None, ALU.add).then_inc(link_pool, 1)
            pool.wait_ge(link_pool, 4)
            g.iota(tab.key_tab[:, 0:CW * s.CA, :], pattern=[[CH, CW], [1, s.CA], [0, s.BATCH]], base=0,
                   channel_multiplier=0, **kw)
            g.iota(tab.key_tab[:, CW * s.CA:M, :], pattern=[[CH, CW], [1, s.CB], [0, s.BATCH]], base=s.CA,
                   channel_multiplier=0, **kw)
            g.iota(tab.lo_tab[:], pattern=[[1, P], [0, s.BATCH]], base=0, channel_multiplier=0, **kw)
            g.memset(acc[:], 0.0)
            pool.wait_ge(rstd_ready, 2)
            pool.wait_ge(x_in, 32)
            for c in range(0, CH, 2):
                g.tensor_scalar(hf[:, c, :], hf[:, c, :], rstd[:, c:c + 1], shift[:, c:c + 1], ALU.mult, ALU.add)

        @block.scalar
        def _(act):
            a = nc.scalar
            dests = [tab.lo, tab.w[0], tab.w[1], tab.w3]

            def copy_expanded(q):
                for k in range(2):
                    act.wait_ge(expanded, 3 + 2 * q + k)
                    a.activation(dests[q][:, k * H2:(k + 1) * H2], ps_e[:, (2 + 2 * q + k) % 6, :],
                                 ACT.Copy).then_inc(copied, 1)

            copy_expanded(0)
            copy_expanded(1)
            act.wait_ge(mv_ready, 1)
            a.activation(std[:], mv[:, :, 1], ACT.Sqrt).then_inc(std_ready, 1)
            copy_expanded(2)
            copy_expanded(3)
            act.wait_ge(rstd_ready, 2)
            act.wait_ge(x_in, 32)
            for c in range(1, CH, 2):
                a.activation(hf[:, c, :], hf[:, c, :], ACT.Identity, bias=shift[:, c:c + 1], scale=rstd[:, c:c + 1])

        @block.vector
        def _(dve):
            v = nc.vector
            count = [0]

            def link(ins):
                count[0] += 1
                ins.then_inc(link_dve, 1)
                dve.wait_ge(link_dve, count[0])

            dve.wait_ge(iotas, 4)
            dve.wait_ge(edges_in, 16 * 9)
            link(v.tensor_copy(dst_f[:], dst_i[:]))
            link(v.tensor_reduce(last_w[:], dst_f[:], AX.X, ALU.max))
            link(v.tensor_scalar(last_w[:], last_w[:], 1.0 / CW, -(CW - 1) / 2.0 / CW, ALU.mult, ALU.add))
            link(v.tensor_scalar(last_w[:], last_w[:], MAGIC, None, ALU.add))
            link(v.tensor_scalar(last_w[:], last_w[:], -MAGIC, None, ALU.add))
            link(v.tensor_scalar(far[:], tile_id[:], float(s.T - 1) - 0.5, BIG, ALU.is_gt, ALU.mult))
            link(v.tensor_tensor(last_w[:], last_w[:], far[:], ALU.add))
            v.tensor_tensor(end_step[:], last_w[:], tile_id[:], ALU.add).then_inc(last_ready, 1)
            dve.wait_ge(last_ready, 1)
            for k in range(TG):
                v.tensor_scalar(passed[:, k, :], step_id[:], end_step[:, k:k + 1], None,
                                ALU.is_gt).then_inc(passed_ready, 1)
            link(v.tensor_scalar(hi_i[:], src_i[:], 7, None, ALU.arith_shift_right))
            link(v.tensor_scalar(lo_i[:], src_i[:], 127, None, ALU.bitwise_and))
            link(v.tensor_copy(hi_f[:], hi_i[:]))
            link(v.tensor_copy(parts[:, 3, :, :], lo_i[:]))
            link(v.scalar_tensor_tensor(key_f[:], dst_f[:], float(CH), hi_f[:], ALU.mult, ALU.add))
            for k, f in ((0, key_f), (4, val)):
                link(v.tensor_copy(parts[:, k, :, :], f[:]))
                link(v.tensor_tensor(rest1[:], f[:], parts[:, k, :, :], ALU.subtract))
                link(v.tensor_copy(parts[:, k + 1, :, :], rest1[:]))
                link(v.tensor_tensor(rest2[:], rest1[:], parts[:, k + 1, :, :], ALU.subtract))
                v.tensor_copy(parts[:, k + 2, :, :], rest2[:]).then_inc(parts_ready, 1)
                dve.wait_ge(parts_ready, 1 + k // 4)
            dve.wait_ge(tiles_counted, 1)
            link(v.tensor_copy(tile_of[:], ps_t[:]))
            for k in range(TG):
                v.tensor_scalar(onehot_t[:, k, :], tile_of[:], tile_id[:, k:k + 1], None,
                                ALU.is_equal).then_inc(hot_ready, 1)
            link(v.tensor_tensor(win_of[:], step_id[:], tile_of[:], ALU.subtract))
            v.memset(tab.same[:, 0:1], 0.0)
            v.tensor_tensor(tab.same[:, 1:ST], tile_of[:, 1:ST], tile_of[:, 0:ST - 1], ALU.subtract)
            dve.wait_ge(x_in, 32)
            for c in range(CH):
                v.bn_stats(stats[:, c, :], hf[:, c, :]).then_inc(stats_ready, 1)
            for k in range(2):
                half = slice(k * H2, (k + 1) * H2)
                dve.wait_ge(expanded, 1 + k)
                link(v.scalar_tensor_tensor(rel[:, half], win_of[:, half], -float(M), ps_e[:, k, :],
                                            ALU.mult, ALU.add))
            v.tensor_scalar(tab.key[:], rel[:], -1.0, float(M), ALU.max, ALU.min).then_inc(key_ready, 1)
            for c in range(CH):
                dve.wait_ge(stats_ready, c + 1)
                ins = v.bn_aggr(mv[:, c, :], stats[:, c, :])
            link(ins)
            v.tensor_scalar(mv[:, :, 1], mv[:, :, 1], 1e-5, None, ALU.add).then_inc(mv_ready, 1)
            dve.wait_ge(std_ready, 1)
            rsqrt(v, link, rstd[:], std[:], mv[:, :, 1], fix[:])
            v.tensor_tensor(rstd[:], rstd[:], fix[:], ALU.mult).then_inc(rstd_ready, 1)
            dve.wait_ge(rstd_ready, 1)
            v.scalar_tensor_tensor(shift[:], mv[:, :, 0], -1.0, rstd[:], ALU.mult, ALU.mult).then_inc(rstd_ready, 1)
            dve.wait_ge(link_pool, 4)
            for k in range(TG):
                v.tensor_scalar(ended[:, k, :], col_w[:], last_w[:, k:k + 1], None, ALU.is_ge).then_inc(ended_ready, 1)
            dve.wait_ge(ended_counted, 1)
            link(v.scalar_tensor_tensor(idx_f[:], ps_t[:, 0:CH], float(CW), node_id[:], ALU.mult, ALU.add))
            link(v.tensor_scalar(idx_f[:], idx_f[:], float(ST * CW - 1), None, ALU.min))
            link(v.tensor_copy(tab.gather[:], idx_f[:]))

        @block.tensor
        def _(pe):
            t = nc.tensor
            pe.wait_ge(passed_ready, TG)
            for k in range(2):
                for g in range(TG):
                    ins = t.matmul(ps_t[:, k * H2:(k + 1) * H2], ones[:, :], passed[:, g, k * H2:(k + 1) * H2],
                                   start=(g == 0), stop=(g == TG - 1))
            ins.then_inc(tiles_counted, 1)
            pe.wait_ge(hot_ready, TG)
            pe.wait_ge(parts_ready, 2)

            def expand(names, slot):
                for k in range(2):
                    for n, (q, g) in enumerate((q, g) for q in names for g in range(TG)):
                        ins = t.matmul(ps_e[:, slot + k, :], parts[:, q, g, :],
                                       onehot_t[:, g, k * H2:(k + 1) * H2], start=(n == 0),
                                       stop=(n == TG * len(names) - 1))
                    ins.then_inc(expanded, 1)

            expand((0, 1, 2), 0)
            expand((3,), 2)
            expand((4,), 4)
            pe.wait_ge(key_ready, 1)
            expand((5,), 0)
            pe.wait_ge(copied, 2)
            expand((6,), 2)
            pe.wait_ge(ended_ready, TG)
            pe.wait_ge(hot_ready, TG)
            for c in range(CH):
                for g in range(TG):
                    ins = t.matmul(ps_t[:, c:c + 1], ended[:, g, c * P:(c + 1) * P], ones[:, 0:1],
                                   start=(g == 0), stop=(g == TG - 1))
            ins.then_inc(ended_counted, 1)


def phase_build(nc, s, tab, a_dram):
    with ExitStack() as ctx:
        def sb(name, shape, dt=F32):
            return ctx.enter_context(nc.sbuf_tensor(name, shape, dt))

        def sem(name):
            return ctx.enter_context(nc.semaphore(name))

        B, M, CW, NB = s.BATCH, s.M, s.CW, s.NB
        Q = B // 4
        PIECES = B // 2
        EARLY = B // 4
        lo_tab, key_tab = tab.lo_tab, tab.key_tab
        lo_hot = sb("lo_hot", [P, 2, P, B], BF16)
        key_hot = sb("key_hot", [P, 2, M, B], BF16)
        key_w = sb("key_w", [P, 2, 3, M, B], BF16)
        w3_b = sb("w3_b", [P, 2, B])
        w1_b = sb("w1_b", [P, 2, EARLY])
        same_b = sb("same_b", [P, 2, B])
        win = sb("win", [P, 2, B, P])
        ps_w = ctx.enter_context(nc.psum_tensor("ps_w", [P, 2, B, P], F32))

        tabs = sem("tabs")
        key_ready = sem("key_ready")
        lo_ready = sem("lo_ready")
        second_ready = sem("second_ready")
        w3_read = sem("w3_read")
        third_ready = sem("third_ready")
        multiplied = sem("multiplied")
        same_ready = sem("same_ready")
        summed = sem("summed")
        stored = [sem(f"stored_{u}") for u in range(2)]

        block = ctx.enter_context(nc.Block())

        def at(b):
            return slice(b * B, (b + 1) * B) if isinstance(b, int) else bass.DynSlice(b * B, B)

        def early(b):
            return slice(b * B, b * B + EARLY) if isinstance(b, int) else bass.DynSlice(b * B, EARLY)

        def later(b):
            return slice(b * B + EARLY, (b + 1) * B) if isinstance(b, int) else bass.DynSlice(b * B + EARLY, B - EARLY)

        def by_scalar(b, j):
            return b * (B + EARLY) + min(2 * j, j + EARLY)

        def late(b, first):
            return not isinstance(b, int) or b >= first

        @block.sync
        def _(sp):
            def store(b, u):
                sp.wait_ge(summed, (b + 1) * B)
                sp.dma_start(a_dram[0][at(b), :, :].rearrange("i p l -> p i l"),
                             win[0:CW * s.CA, u, :, :]).then_inc(stored[u], 16)

            with sp.Fori(0, NB // 2) as it:
                for u in range(2):
                    store(it * 2 + u, u)
            for u in range(2):
                sp.wait_ge(stored[u], 32 * (NB // 2))

        @block.gpsimd
        def _(pool):
            g = nc.gpsimd
            g.memset(win[:, 1, B - 1, :], 0.0).then_inc(tabs, 1)

            def second(b, u):
                if late(b, 2):
                    pool.wait_ge(multiplied, (b - 1) * Q)
                pool.wait_ge(key_ready, (b + 1) * PIECES)
                g.tensor_tensor(key_w[:, u, 1, :, :], key_hot[:, u, :, :],
                                tab.w[1][:, at(b)].unsqueeze(1).broadcast_to([P, M, B]),
                                ALU.mult).then_inc(second_ready, 1)
                g.tensor_tensor(key_w[:, u, 0, :, EARLY:B], key_hot[:, u, :, EARLY:B],
                                tab.w[0][:, later(b)].unsqueeze(1).broadcast_to([P, M, B - EARLY]),
                                ALU.mult).then_inc(second_ready, 1)

            second(0, 0)
            second(1, 1)
            with pool.Fori(1, NB // 2) as it:
                second(it * 2, 0)
                second(it * 2 + 1, 1)

        @block.scalar
        def _(act):
            a = nc.scalar

            def third(b, u):
                if late(b, 2):
                    act.wait_ge(third_ready, by_scalar(b - 1, 0))
                    act.wait_ge(multiplied, (b - 1) * Q)
                a.activation(w3_b[:, u, :], tab.w3[:, at(b)], ACT.Copy).then_inc(w3_read, 1)
                a.activation(w1_b[:, u, :], tab.w[0][:, early(b)], ACT.Copy).then_inc(w3_read, 1)
                act.wait_ge(w3_read, (b + 1) * 2)
                act.wait_ge(key_ready, (b + 1) * PIECES)
                for j in range(B):
                    if j < EARLY:
                        a.activation(key_w[:, u, 0, :, j], key_hot[:, u, :, j], ACT.Copy,
                                     scale=w1_b[:, u, j:j + 1]).then_inc(third_ready, 1)
                    a.activation(key_w[:, u, 2, :, j], key_hot[:, u, :, j], ACT.Copy,
                                 scale=w3_b[:, u, j:j + 1]).then_inc(third_ready, 1)

            def store(b, u):
                act.wait_ge(summed, (b + 1) * B)
                act.dma_start(a_dram[1][at(b), :, :].rearrange("i p l -> p i l"),
                              win[CW * s.CA:M, u, :, :]).then_inc(stored[u], 16)

            third(0, 0)
            third(1, 1)
            store(0, 0)
            with act.Fori(1, NB // 2) as it:
                third(it * 2, 0)
                store(it * 2 - 1, 1)
                third(it * 2 + 1, 1)
                store(it * 2, 0)
            store(NB - 1, 1)

        @block.vector
        def _(dve):
            v = nc.vector

            def mask(b, u, n):
                kind, n = divmod(n, PIECES)
                rows = P if kind else M
                part = slice(n * rows // PIECES, (n + 1) * rows // PIECES)
                shape = [P, part.stop - part.start, B]
                if late(b, 2) and n == 0:
                    if kind == 0:
                        dve.wait_ge(third_ready, by_scalar(b - 1, 0))
                        dve.wait_ge(second_ready, (b - 1) * 2)
                    else:
                        dve.wait_ge(multiplied, (b - 1) * Q)
                if kind == 0:
                    v.tensor_tensor(key_hot[:, u, part, :], key_tab[:, part, :],
                                    tab.key[:, at(b)].unsqueeze(1).broadcast_to(shape),
                                    ALU.is_equal).then_inc(key_ready, 1)
                else:
                    v.tensor_tensor(lo_hot[:, u, part, :], lo_tab[:, part, :],
                                    tab.lo[:, at(b)].unsqueeze(1).broadcast_to(shape),
                                    ALU.is_equal).then_inc(lo_ready, 1)

            def same(b, u):
                if late(b, 2):
                    dve.wait_ge(summed, (b - 1) * B)
                v.tensor_copy(same_b[:, u, :], tab.same[:, at(b)]).then_inc(same_ready, 1)

            def sums(b, u, ahead):
                if ahead:
                    same(b + 1, 1 - u)
                dve.wait_ge(same_ready, b + 1)
                if late(b, 2):
                    dve.wait_ge(stored[u], (b - u) * 16)
                for j in range(B):
                    if j % 4 == 0:
                        dve.wait_ge(multiplied, b * Q + (j // 4 + 1))
                    so_far = win[0:M, u, j - 1, :] if j else win[0:M, 1 - u, B - 1, :]
                    if late(b, 1) or j:
                        dve.wait_ge(summed, b * B + j)
                    v.scalar_tensor_tensor(win[0:M, u, j, :], so_far, same_b[0:M, u, j:j + 1],
                                           ps_w[0:M, u, j, :], ALU.mult, ALU.add).then_inc(summed, 1)
                    if ahead:
                        mask(b + 2, u, j)

            dve.wait_ge(tabs, 1)
            for b in range(2):
                for n in range(2 * PIECES):
                    mask(b, b, n)
            same(0, 0)
            sums(0, 0, True)
            sums(1, 1, True)
            with dve.Fori(1, NB // 2 - 1) as it:
                sums(it * 2, 0, True)
                sums(it * 2 + 1, 1, True)
            same(NB - 1, 1)
            sums(NB - 2, 0, False)
            sums(NB - 1, 1, False)

        @block.tensor
        def _(pe):
            def multiply(b, u):
                pe.wait_ge(lo_ready, (b + 1) * PIECES)
                pe.wait_ge(second_ready, (b + 1) * 2)
                if late(b, 2):
                    pe.wait_ge(summed, (b - 1) * B)
                for j in range(B):
                    pe.wait_ge(third_ready, by_scalar(b, j + 1))
                    for k in range(3):
                        ins = nc.tensor.matmul(ps_w[0:M, u, j, :], key_w[:, u, k, :, j], lo_hot[:, u, :, j],
                                               start=(k == 0), stop=(k == 2))
                    if j % 4 == 3:
                        ins.then_inc(multiplied, 1)

            multiply(0, 0)
            multiply(1, 1)
            with pe.Fori(1, NB // 2) as it:
                for u in range(2):
                    multiply(it * 2 + u, u)


def phase_rounds(nc, s, tab_gather, a_dram, acc, hf, x, x1, moments):
    with ExitStack() as ctx:
        def sb(name, shape, dt=F32):
            return ctx.enter_context(nc.sbuf_tensor(name, shape, dt))

        def sem(name):
            return ctx.enter_context(nc.semaphore(name))

        CH, CA, CB, D = s.CH, s.CA, s.CB, s.D
        SPR = 2 * CH
        RAW = 5
        a_raw = sb("a_raw", [P, RAW, CA * P])
        a_high = sb("a_high", [P, 2, CA * P], F32R)
        a_low = sb("a_low", [P, 2, CA * P], F32R)
        h_high = sb("h_high", [P, CH, D], F32R)
        h_low = sb("h_low", [P, CH, D], F32R)
        squares = sb("squares", [P, D])
        ssq = sb("ssq", [P, CH])
        root = sb("root", [P, CH])
        rinv = sb("rinv", [P, CH])
        fix = sb("fix_h", [P, CH])
        go_tile = sb("go_tile", [P, 1])
        ps = ctx.enter_context(nc.psum_tensor("ps_rows", [P, 16, D], F32))

        gathered = [sem(f"gathered_{u}") for u in range(RAW)]
        high_split = sem("high_split")
        low_split = sem("low_split")
        go = sem("gather_may_start")
        step_done = sem("step_done")
        h_high_ready = sem("h_high_ready")
        h_low_ready = sem("h_low_ready")
        acc_added = sem("acc_added")
        evac_act = sem("evac_act")
        evac_dve = sem("evac_dve")
        squared = sem("squared")
        clamped = sem("clamped")
        rooted = sem("rooted")
        link_dve = sem("link_norm")
        scaled = sem("scaled")
        x_in = sem("x_again_in")
        x1_cleared = sem("x1_cleared")
        x1_ready = sem("x1_ready")
        LINKS = 10
        NEXT = CH + 11
        START = NEXT + CA + 12 - SPR

        block = ctx.enter_context(nc.Block())
        chunks = [range(0, CA), range(CA, CH)]
        banks = [[(n // 2, r[n], min(2, len(r) - n)) for n in range(0, len(r), 2)] for r in chunks]
        even = [[b for b in bs if b[0] % 2 == 0] for bs in banks]
        odd = [[b for b in bs if b[0] % 2] for bs in banks]
        n_even, n_odd = sum(map(len, even)), sum(map(len, odd))
        width = [CA * P, CB * P]

        def pass_of(k):
            return (k % SPR) // CH

        @block.sync
        def _(sp):
            sp.wait_ge(step_done, 8)
            full, tail = rows_of(x, s)
            sp.dma_start(x1[:, 0:s.FULL, :], full).then_inc(x_in, 16)
            sp.wait_ge(x1_cleared, 1)
            sp.dma_start(x1[0:s.REST, s.FULL, :], tail).then_inc(x_in, 16)
            sp.wait_ge(x_in, 32)

        @block.gpsimd
        def _(pool):
            g = nc.gpsimd

            def gather(step, k):
                if not isinstance(step, int) or step >= RAW:
                    pool.wait_ge(low_split, step - (RAW - 1))
                    pool.wait_ge(go, step - (RAW - 1))
                    g.tensor_tensor(go_tile[:], go_tile[:], go_tile[:], ALU.add).then_inc(go, 1)
                which = pass_of(k)
                g.indirect_dma_start(
                    out=a_raw[:, k % RAW, 0:width[which]], out_offset=None,
                    in_=a_dram[which].rearrange("i (c r) l -> (i c) (r l)", c=s.CW),
                    in_offset=bass.IndirectOffsetOnAxis(ap=tab_gather[:, k % CH:k % CH + 1], axis=0),
                ).then_inc(gathered[k % RAW], 16)

            g.memset(go_tile[:], 0.0).then_inc(go, 1)
            def run(layer, last):
                for k in range(RAW, SPR if last else SPR + RAW):
                    gather(layer * SPR + k, k)
                    for c in range(3 * (k - 6), min(3 * (k - 5), CH)):
                        if c >= 0:
                            pool.wait_ge(scaled, layer * CH + (c + 1))
                            g.tensor_tensor(acc[:, c, :], acc[:, c, :], hf[:, c, :], ALU.add).then_inc(acc_added, 1)

            for k in range(RAW):
                gather(k, k)
            g.memset(x1[:, s.FULL, :], 0.0).then_inc(x1_cleared, 1)
            with pool.Fori(0, s.LAYERS - 1) as layer:
                run(layer, False)
            run(s.LAYERS - 1, True)

        @block.scalar
        def _(act):
            a = nc.scalar

            def high(layer, k):
                u, n, step = k % 2, width[pass_of(k)], layer * SPR + k
                act.wait_ge(gathered[k % RAW], (layer * (SPR // RAW) + (k // RAW + 1)) * 16)
                if not isinstance(step, int) or step >= 2:
                    act.wait_ge(step_done, step - 1)
                a.activation(a_high[:, u, 0:n], a_raw[:, k % RAW, 0:n], ACT.Copy).then_inc(high_split, 1)

            def h_high_of(layer, c):
                act.wait_ge(scaled, layer * CH + (c + 1))
                a.activation(h_high[:, c, :], hf[:, c, :], ACT.Copy).then_inc(h_high_ready, 1)

            def evacuate(layer, w):
                act.wait_ge(step_done, layer * SPR + CH * (w + 1))
                if w == 0:
                    act.wait_ge(h_low_ready, layer * CH + CH)
                    act.wait_ge(acc_added, layer * CH + CH)
                for bank, c, n in even[w]:
                    a.activation(hf[:, c:c + n, :], ps[:, 2 * bank:2 * bank + n, :], ACT.Copy).then_inc(evac_act, 1)

            def square(layer, w, cs):
                act.wait_ge(evac_act, (layer + 1) * n_even + sum(map(len, even[:w + 1])))
                act.wait_ge(evac_dve, (layer + 1) * n_odd + sum(map(len, odd[:w + 1])))
                for c in cs:
                    if c:
                        act.wait_ge(squared, layer * CH + c)
                    a.activation(squares[:], hf[:, c, :], ACT.Square, accum_out=ssq[:, c:c + 1]).then_inc(squared, 1)

            def roots(layer, w):
                act.wait_ge(clamped, layer * 2 + (w + 1))
                r = slice(chunks[w][0], chunks[w][-1] + 1)
                a.activation(root[:, r], ssq[:, r], ACT.Sqrt).then_inc(rooted, 1)

            def split(layer, k0, k1):
                for k in range(k0, k1):
                    high(layer, k)

            def run(layer, last):
                split(layer, START, CH + 1)
                evacuate(layer, 0)
                for n in range(5):
                    split(layer, CH + 1 + n, CH + 2 + n)
                    square(layer, 0, range(3 * n, 3 * n + 3))
                roots(layer, 0)
                split(layer, CH + 6, NEXT)
                if last:
                    split(layer, NEXT, SPR)
                    evacuate(layer, 1)
                    square(layer, 1, chunks[1])
                    roots(layer, 1)
                    return
                for c in chunks[0]:
                    split(layer, NEXT + c, NEXT + c + 1)
                    act.wait_ge(step_done, layer * SPR + (CH + c + 1))
                    h_high_of(layer + 1, c)
                evacuate(layer, 1)
                split(layer, SPR + 1, SPR + 2)
                for n in range(5):
                    split(layer, SPR + 2 + n, SPR + 3 + n)
                    square(layer, 1, range(CA + 2 * n, CA + 2 * n + 2))
                roots(layer, 1)
                split(layer, SPR + 7, SPR + 9)
                for n in range(4):
                    split(layer, SPR + 9 + n, SPR + 10 + n)
                    for c in range(CA + 3 * n, min(CA + 3 * n + 3, CH)):
                        h_high_of(layer + 1, c)

            act.sem_inc(evac_act, n_even)
            h_high_of(0, 0)
            high(0, 0)
            high(0, 1)
            for k in range(2, START):
                for c in range(3 * k - 5, min(3 * k - 2, CH)):
                    h_high_of(0, c)
                high(0, k)
            with act.Fori(0, s.LAYERS - 1) as layer:
                run(layer, False)
            run(s.LAYERS - 1, True)

        @block.vector
        def _(dve):
            v = nc.vector

            def low(layer, k):
                u, n, step = k % 2, width[pass_of(k)], layer * SPR + k
                dve.wait_ge(high_split, step + 1)
                v.tensor_tensor(a_low[:, u, 0:n], a_raw[:, k % RAW, 0:n], a_high[:, u, 0:n].bitcast(F32),
                                ALU.subtract).then_inc(low_split, 1)

            def h_low_of(layer, c):
                dve.wait_ge(h_high_ready, layer * CH + (c + 1))
                v.tensor_tensor(h_low[:, c, :], hf[:, c, :], h_high[:, c, :].bitcast(F32),
                                ALU.subtract).then_inc(h_low_ready, 1)

            def evacuate(layer, w):
                dve.wait_ge(step_done, layer * SPR + CH * (w + 1))
                if w == 0:
                    dve.wait_ge(h_low_ready, layer * CH + CH)
                    dve.wait_ge(acc_added, layer * CH + CH)
                for bank, c, n in odd[w]:
                    v.tensor_copy(hf[:, c:c + n, :], ps[:, 2 * bank:2 * bank + n, :]).then_inc(evac_dve, 1)

            def inverse(layer, w, last):
                r = slice(chunks[w][0], chunks[w][-1] + 1)
                n = [w * LINKS // 2]

                def link(ins):
                    n[0] += 1
                    ins.then_inc(link_dve, 1)
                    dve.wait_ge(link_dve, layer * LINKS + n[0])

                dve.wait_ge(squared, layer * CH + chunks[w][-1] + 1)
                v.tensor_scalar(ssq[:, r], ssq[:, r], 1e-24, None, ALU.max).then_inc(clamped, 1)
                dve.wait_ge(rooted, layer * 2 + (w + 1))
                rsqrt(v, link, rinv[:, r], root[:, r], ssq[:, r], fix[:, r])
                link(v.scalar_tensor_tensor(rinv[:, r], rinv[:, r], 1.0 / (s.LAYERS + 1) if last else 1.0,
                                            fix[:, r], ALU.mult, ALU.mult))

            def scale(cs):
                for c in cs:
                    v.tensor_scalar(hf[:, c, :], hf[:, c, :], rinv[:, c:c + 1], None, ALU.mult).then_inc(scaled, 1)

            def split(layer, k0, k1):
                for k in range(k0, k1):
                    low(layer, k)

            def add_sum(cs):
                for c in cs:
                    dve.wait_ge(acc_added, (s.LAYERS - 1) * CH + (c + 1))
                    v.scalar_tensor_tensor(x1[:, c, :], acc[:, c, :], 1.0 / (s.LAYERS + 1), x1[:, c, :],
                                           ALU.mult, ALU.add).then_inc(x1_ready, 1)

            def add_last(cs):
                for c in cs:
                    dve.wait_ge(x1_ready, c + 1)
                    v.scalar_tensor_tensor(x1[:, c, :], hf[:, c, :], rinv[:, c:c + 1], x1[:, c, :],
                                           ALU.mult, ALU.add).then_inc(x1_ready, 1)
                for c in cs:
                    dve.wait_ge(x1_ready, CH + c + 1)
                    v.bn_stats(moments[:, c, :], x1[:, c, :])

            def run(layer, last):
                if last:
                    dve.wait_ge(x_in, 32)
                    for n in range(CH + 1 - START):
                        split(layer, START + n, START + n + 1)
                        add_sum(range(3 * n, min(3 * n + 3, CH)))
                else:
                    split(layer, START, CH + 1)
                evacuate(layer, 0)
                split(layer, CH + 1, CH + 6)
                inverse(layer, 0, last)
                for n in range(5):
                    split(layer, CH + 6 + n, CH + 7 + n)
                    (add_last if last else scale)(range(3 * n, 3 * n + 3))
                if last:
                    split(layer, NEXT, SPR)
                    evacuate(layer, 1)
                    inverse(layer, 1, last)
                    add_last(chunks[1])
                    return
                for c in chunks[0]:
                    split(layer, NEXT + c, NEXT + c + 1)
                    h_low_of(layer + 1, c)
                evacuate(layer, 1)
                split(layer, SPR + 1, SPR + 2)
                split(layer, SPR + 2, SPR + 7)
                inverse(layer, 1, last)
                for n in range(2):
                    split(layer, SPR + 7 + n, SPR + 8 + n)
                    scale(range(CA + CB // 2 * n, CA + CB // 2 * (n + 1)))
                for n in range(4):
                    split(layer, SPR + 9 + n, SPR + 10 + n)
                    for c in range(CA + 3 * n, min(CA + 3 * n + 3, CH)):
                        h_low_of(layer + 1, c)

            dve.sem_inc(scaled, CH)
            dve.sem_inc(evac_dve, n_odd)
            h_low_of(0, 0)
            low(0, 0)
            low(0, 1)
            for k in range(2, START):
                for c in range(3 * k - 5, min(3 * k - 2, CH)):
                    h_low_of(0, c)
                low(0, k)
            with dve.Fori(0, s.LAYERS - 1) as layer:
                run(layer, False)
            run(s.LAYERS - 1, True)

        @block.tensor
        def _(pe):
            def step(n, k, c, first, last, layer):
                u, w = k % 2, pass_of(k)
                pe.wait_ge(low_split, n + 1)
                if w == 0:
                    pe.wait_ge(h_low_ready, layer * CH + (c + 1))
                for r in range(len(chunks[w])):
                    if first and r % 2 == 0 and (w == 1 or r < CB):
                        bank = r // 2
                        evac, mine = (evac_dve, odd) if bank % 2 else (evac_act, even)
                        per = len(mine[0]) + len(mine[1])
                        pe.wait_ge(evac, layer * per + ((per if w else len(mine[0])) + bank // 2 + 1))
                    block_r = slice(r * P, (r + 1) * P)
                    for m, (a_part, h_part) in enumerate(((a_high, h_high), (a_high, h_low), (a_low, h_high))):
                        rhs = h_part[:, c, :] if isinstance(c, int) else \
                            h_part[:, bass.DynSlice(c, 1), :].rearrange("p c d -> p (c d)")
                        ins = nc.tensor.matmul(ps[:, r, :], a_part[:, u, block_r], rhs,
                                               start=(first and m == 0 and r % 2 == 0), stop=(last and m == 2),
                                               skip_group_check=True)
                ins.then_inc(step_done, 1)

            with pe.Fori(0, s.LAYERS) as layer:
                for w in range(2):
                    k0 = w * CH
                    step(layer * SPR + k0, k0, 0, True, False, layer)
                    with pe.Fori(0, (CH - 3) // 2) as j:
                        for t in (1, 2):
                            step(layer * SPR + (j * 2 + (k0 + t)), k0 + t, j * 2 + t, False, False, layer)
                    for c in (CH - 2, CH - 1):
                        step(layer * SPR + (k0 + c), k0 + c, c, False, c == CH - 1, layer)


def phase_route(nc, s, moments, x1, y, gate_w, gate_b, b1, beta, routes, y_dram, x1_dram):
    with ExitStack() as ctx:
        def sb(name, shape, dt=F32):
            return ctx.enter_context(nc.sbuf_tensor(name, shape, dt))

        def sem(name):
            return ctx.enter_context(nc.semaphore(name))

        CH, D, E, MT, F4 = s.CH, s.D, s.E, s.MT, s.F // P
        NS = MT * s.TB // P
        AHEAD = 6
        K2 = 2 * CH
        KD = D // P
        mv = sb("mv_y", [P, CH, 2])
        std = sb("std_y", [P, CH])
        rstd = sb("rstd_y", [P, CH])
        fix = sb("fix_y", [P, CH])
        shift = sb("shift_y", [P, CH])
        ident = sb("ident", [P, P])
        yT = sb("yT", [P, 4, KD, P])
        gw = sb("gw", [P, KD, E])
        gb = sb("gb", [P, E])
        bt = sb("bt", [P, D])
        b1_sb = sb("b1_sb", [E, s.F])
        logits = sb("logits", [P, CH, E])
        top = sb("top", [P, CH, 8])
        top_i = sb("top_i", [P, CH, 8], U32)
        gap = sb("gap", [P, CH])
        ex = sb("ex", [P, CH])
        den = sb("den", [P, CH])
        choice = sb("choice", [P, 2, CH])
        node_id = sb("node_id2", [P, CH])
        absent = sb("absent", [P, CH])
        e_row = sb("e_row", [P, E])
        e_part = sb("e_part", [P, 1])
        t_row = sb("t_row", [P, MT])
        all_ones = sb("all_ones", [P, E * K2])
        ones_b = sb("ones_b", [P, P], BF16)
        below = sb("below", [P, P], BF16)
        chosen = sb("chosen", [P, E, K2])
        running = sb("running", [P, E, K2])
        place = sb("place", [P, E, K2])
        count_f = sb("count_f", [P, E])
        count_b = sb("count_b", [P, E], BF16)
        prior = sb("prior", [P, E])
        n_tiles = sb("n_tiles", [P, E])
        tile_end = sb("tile_end", [P, E])
        base = sb("base", [P, E])
        pos_f = sb("pos_f", [P, K2])
        past = sb("past", [P, MT, E])
        expert_f = sb("expert_f", [P, MT])
        expert_hot = sb("expert_hot", [P, MT])
        place_i = sb("place_i", [P, K2], I32)
        hi_i = sb("place_hi_i", [P, K2], I32)
        lo_i = sb("place_lo_i", [P, K2], I32)
        hi_b = sb("place_hi", [P, K2], BF16)
        lo_b = sb("place_lo", [P, K2], BF16)
        chunk_no = sb("chunk_no", [P, 2, CH], BF16)
        lo_tab = sb("lo_tab_s", [P, P, K2], BF16)
        hi_tab = sb("hi_tab_s", [P, NS, K2], BF16)
        lo_hot = sb("lo_hot_s", [P, P, K2], BF16)
        hi_hot = sb("hi_hot_s", [P, NS, K2], BF16)
        hi_no = sb("hi_no_s", [P, 2, NS, K2], BF16)
        slot_part = sb("slot_part", [P, NS])
        ps_s = ctx.enter_context(nc.psum_tensor("ps_s", [P, 512], F32))
        ps_y = ctx.enter_context(nc.psum_tensor("ps_y", [P, 4, 4, P], F32))
        ps_l = ctx.enter_context(nc.psum_tensor("ps_l", [P, 512], F32))
        ps_c = ctx.enter_context(nc.psum_tensor("ps_c", [P, 512], F32))
        ps_b = ctx.enter_context(nc.psum_tensor("ps_b", [P, 512], F32))

        consts_in = sem("consts_in")
        tabs = sem("tabs_y")
        link_dve = sem("link_y")
        beta_added = sem("beta_added")
        y_stored = sem("y_stored")
        mv_ready = sem("mv_y_ready")
        std_ready = sem("std_y_ready")
        shift_ready = sem("shift_ready")
        y_even = sem("y_even")
        y_odd = sem("y_odd")
        turned = sem("turned")
        turned_even = sem("turned_even")
        turned_odd = sem("turned_odd")
        gated = sem("gated")
        topped = sem("topped")
        exp_ready = sem("exp_ready")
        gap_ready = sem("gap_ready")
        counts = sem("counts")
        counted = sem("counted")
        hot_ready = sem("expert_hot_ready")
        b1_ready = sem("b1_ready")
        hi_hot_ready = sem("hi_hot_ready")
        split_ready = sem("place_split")
        numbered = sem("partition_numbers")
        slots_ready = sem("slots_ready")

        block = ctx.enter_context(nc.Block())

        @block.sync
        def _(sp):
            sp.dma_start(gw[:, :, :], gate_w.rearrange("(k p) e -> p k e", p=P)).then_inc(consts_in, 16)
            sp.dma_start(gb[:, :], gate_b.rearrange("(a e) -> a e", a=1).broadcast_to([P, E])).then_inc(consts_in, 16)
            sp.dma_start(bt[:, :], beta.rearrange("(a e) -> a e", a=1).broadcast_to([P, D])).then_inc(consts_in, 16)
            sp.dma_start(b1_sb[:, :], b1).then_inc(consts_in, 16)
            full, tail = rows_of(y_dram, s)
            G = s.FULL // 4
            for n in range(4):
                sp.wait_ge(y_even, -(-(n + 1) * G // 2))
                sp.wait_ge(y_odd, (n + 1) * G // 2)
                sp.dma_start(full[:, n * G:(n + 1) * G, :], y[:, n * G:(n + 1) * G, :]).then_inc(y_stored, 16)
            sp.wait_ge(y_even, (CH + 1) // 2)
            sp.dma_start(tail, y[0:s.REST, s.FULL, :]).then_inc(y_stored, 16)
            full, tail = rows_of(x1_dram, s)
            sp.wait_ge(beta_added, s.FULL)
            sp.dma_start(full, x1[:, 0:s.FULL, :]).then_inc(y_stored, 16)
            sp.wait_ge(beta_added, CH)
            sp.dma_start(tail, x1[0:s.REST, s.FULL, :]).then_inc(y_stored, 16)
            sp.wait_ge(y_stored, 16 * 7)

        @block.gpsimd
        def _(pool):
            g = nc.gpsimd
            kw = dict(allow_small_or_imprecise_dtypes=True)
            g.memset(all_ones[:], 1.0).then_inc(tabs, 1)
            g.memset(ones_b[:], 1.0).then_inc(tabs, 1)
            pool.wait_ge(tabs, 2)
            g.affine_select(out=ident[:], in_=all_ones[:, 0:P], pattern=[[1, P]], compare_op=ALU.is_equal,
                            fill=0.0, base=0, channel_multiplier=-1).then_inc(tabs, 1)
            g.affine_select(out=below[:], in_=ones_b[:], pattern=[[1, P]], compare_op=ALU.is_gt,
                            fill=0.0, base=0, channel_multiplier=-1).then_inc(tabs, 1)
            g.iota(node_id[:], pattern=[[P, CH]], base=0, channel_multiplier=1, **kw).then_inc(tabs, 1)
            g.iota(e_row[:], pattern=[[1, E]], base=0, channel_multiplier=0, **kw).then_inc(tabs, 1)
            g.iota(e_part[:], pattern=[[0, 1]], base=0, channel_multiplier=1, **kw).then_inc(tabs, 1)
            g.iota(t_row[:], pattern=[[1, MT]], base=0, channel_multiplier=0, **kw).then_inc(tabs, 1)
            g.iota(lo_tab[:], pattern=[[1, P], [0, K2]], base=0, channel_multiplier=0, **kw).then_inc(tabs, 1)
            g.iota(hi_tab[:], pattern=[[1, NS], [0, K2]], base=0, channel_multiplier=0, **kw).then_inc(tabs, 1)
            g.iota(chunk_no[:], pattern=[[0, 2], [1, CH]], base=0, channel_multiplier=0, **kw).then_inc(tabs, 1)
            pool.wait_ge(consts_in, 64)
            for c in range(CH):
                pool.wait_ge((y_odd if c % 2 else y_even), c // 2 + 1)
                g.tensor_tensor(x1[:, c, :], x1[:, c, :], bt[:], ALU.add).then_inc(beta_added, 1)

        @block.scalar
        def _(act):
            a = nc.scalar
            act.wait_ge(mv_ready, 1)
            a.activation(std[:], mv[:, :, 1], ACT.Sqrt).then_inc(std_ready, 1)
            act.wait_ge(shift_ready, 1)

            def copy_turned(c):
                act.wait_ge(turned, c + 1)
                if c >= 4:
                    act.wait_ge(gated, c - 3)
                a.activation(yT[:, c % 4, :, :], ps_y[:, c % 4, 0:KD, :], ACT.Copy).then_inc(turned_even, 1)

            for c in range(0, CH + AHEAD, 2):
                if c < CH:
                    a.activation(y[:, c, :], x1[:, c, :], ACT.Identity, bias=shift[:, c:c + 1],
                                 scale=rstd[:, c:c + 1]).then_inc(y_even, 1)
                if c >= AHEAD and c - AHEAD < CH:
                    copy_turned(c - AHEAD)
            act.wait_ge(gap_ready, 1)
            a.activation(ex[:], gap[:], ACT.Exp).then_inc(exp_ready, 1)
            for k in range(2):
                act.wait_ge(hi_hot_ready, k + 1)
                js = slice(k * CH, (k + 1) * CH)
                a.activation(hi_no[:, 1, :, js], hi_hot[:, :, js], ACT.Copy, scale=e_part[:]).then_inc(numbered, 1)
            act.wait_ge(b1_ready, 1)
            a.activation(routes.b1[:].rearrange("p t f -> p f t"),
                         ps_b[:, 0:F4 * MT].rearrange("p (f t) -> p f t", t=MT), ACT.Copy)

        @block.vector
        def _(dve):
            v = nc.vector
            n_link = [0]

            def link(ins):
                n_link[0] += 1
                ins.then_inc(link_dve, 1)
                dve.wait_ge(link_dve, n_link[0])

            def copy_turned(c):
                dve.wait_ge(turned, c + 1)
                if c >= 4:
                    dve.wait_ge(gated, c - 3)
                v.tensor_copy(yT[:, c % 4, :, :], ps_y[:, c % 4, 0:KD, :]).then_inc(turned_odd, 1)

            for c in range(CH):
                ins = v.bn_aggr(mv[:, c, :], moments[:, c, :])
            link(ins)
            v.tensor_scalar(mv[:, :, 1], mv[:, :, 1], 1e-5, None, ALU.add).then_inc(mv_ready, 1)
            dve.wait_ge(mv_ready, 1)
            dve.wait_ge(std_ready, 1)
            rsqrt(v, link, rstd[:], std[:], mv[:, :, 1], fix[:])
            link(v.tensor_tensor(rstd[:], rstd[:], fix[:], ALU.mult))
            v.scalar_tensor_tensor(shift[:], mv[:, :, 0], -1.0, rstd[:], ALU.mult, ALU.mult).then_inc(shift_ready, 1)
            dve.wait_ge(shift_ready, 1)
            for c in range(1, CH + AHEAD, 2):
                if c < CH:
                    v.tensor_scalar(y[:, c, :], x1[:, c, :], rstd[:, c:c + 1], shift[:, c:c + 1],
                                    ALU.mult, ALU.add).then_inc(y_odd, 1)
                if c >= AHEAD + 1 and c - AHEAD < CH:
                    copy_turned(c - AHEAD)
            dve.wait_ge(consts_in, 64)
            dve.wait_ge(gated, CH)
            link(v.tensor_tensor(logits[:], ps_l[:, 0:CH * E].rearrange("p (c e) -> p c e", e=E),
                                 gb[:].unsqueeze(1).broadcast_to([P, CH, E]), ALU.add))
            for c in range(CH):
                v.max(top[:, c, :], logits[:, c, :]).then_inc(topped, 1)
            for c in range(CH):
                dve.wait_ge(topped, c + 1)
                ins = v.max_index(top_i[:, c, :], top[:, c, :], logits[:, c, :])
            link(ins)
            v.tensor_tensor(gap[:], top[:, :, 1], top[:, :, 0], ALU.subtract).then_inc(gap_ready, 1)
            dve.wait_ge(tabs, 11)
            link(v.tensor_scalar(absent[:], node_id[:], float(s.N) - 0.5, 100.0, ALU.is_gt, ALU.mult))
            for k in range(2):
                link(v.tensor_copy(choice[:, k, :], top_i[:, :, k]))
                link(v.tensor_tensor(choice[:, k, :], choice[:, k, :], absent[:], ALU.add))
            flat = choice[:].rearrange("p k c -> p (k c)")
            link(v.tensor_tensor(chosen[:], flat.unsqueeze(1).broadcast_to([P, E, K2]),
                                 e_row[:].unsqueeze(2).broadcast_to([P, E, K2]), ALU.is_equal))
            flat = chosen[:].rearrange("p e j -> p (e j)")
            link(v.tensor_tensor_scan(running[:].rearrange("p e j -> p (e j)"), all_ones[:], flat, 0.0,
                                      ALU.mult, ALU.add))
            link(v.memset(prior[:, 0:1], 0.0))
            link(v.tensor_copy(prior[:, 1:E], running[:, 0:E - 1, K2 - 1]))
            link(v.tensor_tensor(count_f[:], running[:, :, K2 - 1], prior[:], ALU.subtract))
            v.tensor_copy(count_b[:], count_f[:]).then_inc(counts, 1)
            dve.wait_ge(exp_ready, 1)
            link(v.tensor_scalar(den[:], ex[:], 1.0, None, ALU.add))
            link(v.reciprocal(routes.weight[:, 0, :], den[:]))
            link(v.tensor_tensor(routes.weight[:, 1, :], ex[:], routes.weight[:, 0, :], ALU.mult))
            dve.wait_ge(counted, 1)
            link(v.tensor_scalar(n_tiles[:], ps_c[:, 0:E], 1.0 / s.TB, (s.TB - 1) / 2.0 / s.TB, ALU.mult, ALU.add))
            link(v.tensor_scalar(n_tiles[:], n_tiles[:], MAGIC, None, ALU.add))
            link(v.tensor_scalar(n_tiles[:], n_tiles[:], -MAGIC, None, ALU.add))
            link(v.tensor_tensor_scan(tile_end[:], all_ones[:, 0:E], n_tiles[:], 0.0, ALU.mult, ALU.add))
            link(v.tensor_tensor(base[:], tile_end[:], n_tiles[:], ALU.subtract))
            link(v.scalar_tensor_tensor(base[:], base[:], float(s.TB), ps_c[:, E:2 * E], ALU.mult, ALU.add))
            link(v.scalar_tensor_tensor(base[:], base[:], -1.0, prior[:], ALU.add, ALU.subtract))
            link(v.tensor_tensor(place[:], running[:], base[:].unsqueeze(2).broadcast_to([P, E, K2]), ALU.add))
            link(v.tensor_tensor(place[:], place[:], chosen[:], ALU.mult))
            link(v.tensor_reduce(pos_f[:], place[:].rearrange("p e j -> p j e"), AX.X, ALU.add))
            link(v.tensor_copy(routes.place[:], pos_f[:]))
            link(v.tensor_copy(place_i[:], pos_f[:]))
            link(v.tensor_scalar(hi_i[:], place_i[:], 7, None, ALU.arith_shift_right))
            link(v.tensor_scalar(lo_i[:], place_i[:], 127, None, ALU.bitwise_and))
            link(v.tensor_copy(hi_b[:], hi_i[:]))
            link(v.tensor_copy(lo_b[:], lo_i[:]))
            link(v.tensor_tensor(hi_b[:].rearrange("p (k c) -> p k c", k=2), hi_b[:].rearrange("p (k c) -> p k c", k=2),
                                 absent[:].unsqueeze(1).broadcast_to([P, 2, CH]), ALU.add))
            for k in range(2):
                js = slice(k * CH, (k + 1) * CH)
                v.tensor_tensor(hi_hot[:, :, js], hi_tab[:, :, js], hi_b[:, js].unsqueeze(1).broadcast_to([P, NS, CH]),
                                ALU.is_equal).then_inc(hi_hot_ready, 1)
                v.tensor_tensor(lo_hot[:, :, js], lo_tab[:, :, js], lo_b[:, js].unsqueeze(1).broadcast_to([P, P, CH]),
                                ALU.is_equal).then_inc(split_ready, 1)
                dve.wait_ge(hi_hot_ready, k + 1)
                v.tensor_tensor(hi_no[:, 0, :, js], hi_hot[:, :, js],
                                chunk_no[:, k, :].unsqueeze(1).broadcast_to([P, NS, CH]),
                                ALU.mult).then_inc(split_ready, 1)
            link(v.tensor_tensor(past[:], t_row[:].unsqueeze(2).broadcast_to([P, MT, E]),
                                 tile_end[:].unsqueeze(1).broadcast_to([P, MT, E]), ALU.is_ge))
            link(v.tensor_reduce(expert_f[:], past[:], AX.X, ALU.add))
            link(v.tensor_scalar(expert_f[:], expert_f[:], float(E - 1), None, ALU.min))
            link(v.tensor_copy(routes.expert[:], expert_f[:]))
            v.tensor_scalar(expert_hot[:], expert_f[:], e_part[:], None, ALU.is_equal).then_inc(hot_ready, 1)
            dve.wait_ge(slots_ready, 1)
            link(v.tensor_copy(slot_part[:], ps_s[:, NS:2 * NS]))
            v.scalar_tensor_tensor(routes.token[:], ps_s[:, 0:NS], float(P), slot_part[:], ALU.mult, ALU.add)

        @block.tensor
        def _(pe):
            t = nc.tensor
            pe.wait_ge(tabs, 4)
            pe.wait_ge(consts_in, 64)

            def gate(c):
                pe.wait_ge((turned_odd if c % 2 else turned_even), c // 2 + 1)
                for k in range(KD):
                    ins = t.matmul(ps_l[:, c * E:(c + 1) * E], yT[:, c % 4, k, :], gw[:, k, :],
                                   start=(k == 0), stop=(k == KD - 1))
                ins.then_inc(gated, 1)

            for c in range(CH):
                pe.wait_ge((y_odd if c % 2 else y_even), c // 2 + 1)
                if c >= 4:
                    pe.wait_ge((turned_odd if c % 2 else turned_even), (c - 4) // 2 + 1)
                for k in range(KD):
                    ins = t.transpose(ps_y[:, c % 4, k, :], y[:, c, k * P:(k + 1) * P], ident[:, :])
                ins.then_inc(turned, 1)
                if c >= 2:
                    gate(c - 2)
            gate(CH - 2)
            gate(CH - 1)
            pe.wait_ge(counts, 1)
            t.matmul(ps_c[:, 0:E], ones_b[:, :], count_b[:, :], start=True, stop=True)
            t.matmul(ps_c[:, E:2 * E], below[:, :], count_b[:, :], start=True, stop=True).then_inc(counted, 1)
            for j in range(K2):
                if j % CH == 0:
                    pe.wait_ge(split_ready, 2 * (j // CH + 1))
                    pe.wait_ge(numbered, j // CH + 1)
                ins = t.matmul(ps_s[:, 0:2 * NS], lo_hot[:, :, j], hi_no[:, :, :, j].rearrange("p a b -> p (a b)"),
                               start=(j == 0), stop=(j == K2 - 1))
            ins.then_inc(slots_ready, 1)
            pe.wait_ge(hot_ready, 1)
            for f in range(F4):
                ins = t.matmul(ps_b[:, f * MT:(f + 1) * MT], b1_sb[:, f * P:(f + 1) * P], expert_hot[0:E, :],
                               start=True, stop=True)
            ins.then_inc(b1_ready, 1)


class Routes:

    def __init__(self, nc, ctx, s):
        def sb(name, shape, dt=F32):
            return ctx.enter_context(nc.sbuf_tensor(name, shape, dt))

        self.place = sb("r_place", [P, 2 * s.CH], U32)
        self.weight = sb("r_weight", [P, 2, s.CH])
        self.token = sb("r_token", [P, s.MT * s.TB // P], U32)
        self.expert = sb("r_expert", [P, s.MT], I32)
        self.b1 = sb("r_b1", [P, s.MT, s.F // P])


def phase_experts(nc, s, routes, w1, w2, b2, y_dram, ys_dram):
    with ExitStack() as ctx:
        def sb(name, shape, dt=F32):
            return ctx.enter_context(nc.sbuf_tensor(name, shape, dt))

        def sem(name):
            return ctx.enter_context(nc.semaphore(name))

        D, F, MT, TB = s.D, s.F, s.MT, s.TB
        KD, KF, HALVES = D // P, F // P, TB // P
        WN = KD * F
        w_raw = [sb(f"w{n}_raw", [P, s.E, WN]) for n in (1, 2)]
        w_high = [sb(f"w{n}_high", [P, 2, WN], F32R) for n in (1, 2)]
        w_low = [sb(f"w{n}_low", [P, 2, WN], F32R) for n in (1, 2)]
        b2_t = sb("b2_t", [P, 2, D])
        x_t = sb("x_t", [P, 2, HALVES, D])
        token_t = sb("token_t", [P, 2, HALVES], U32)
        go_tile = sb("go_tile_e", [P, 1])
        x_high = sb("x_high", [P, 2, KD, TB], F32R)
        x_low = sb("x_low", [P, 2, KD, TB], F32R)
        b1_t = sb("b1_t", [P, 2, KF])
        hid = sb("hid", [P, 2, KF, TB])
        hid_high = sb("hid_high", [P, 2, KF, TB], F32R)
        hid_low = sb("hid_low", [P, 2, KF, TB], F32R)
        y_t = sb("y_t", [P, 2, HALVES, D])
        ones = sb("ones_e", [P, P])
        ident = sb("ident_e", [P, P])
        ps_x = ctx.enter_context(nc.psum_tensor("ps_x", [P, 2, KD, TB], F32))
        ps_h = ctx.enter_context(nc.psum_tensor("ps_h", [P, 2, KF, TB], F32))
        ps_o = ctx.enter_context(nc.psum_tensor("ps_o", [P, 2, HALVES, D], F32))

        x_loaded = [sem(f"tokens_in_{u}") for u in range(2)]
        y_stored = [sem(f"results_out_{u}") for u in range(2)]
        w_loaded = sem("weights_in")
        b2_loaded = [sem(f"b2_in_{u}") for u in range(2)]
        tabs = sem("ident_ready")
        token_ready = sem("token_ready")
        go = sem("collect_may_start")
        w_high_ready = [sem(f"w{n}_high_ready") for n in (1, 2)]
        w_low_ready = [sem(f"w{n}_low_ready") for n in (1, 2)]
        x_turned = sem("x_turned")
        x_high_ready = sem("x_high_ready")
        x_low_ready = sem("x_low_ready")
        first_done = sem("first_done")
        b1_ready = sem("b1_t_ready")
        hid_ready = sem("hid_ready")
        hid_high_ready = sem("hid_high_ready")
        hid_low_ready = sem("hid_low_ready")
        second_done = sem("second_done")
        y_ready = sem("y_ready")

        block = ctx.enter_context(nc.Block())

        def late(t, first):
            return not isinstance(t, int) or t >= first

        def one(t):
            return slice(t, t + 1) if isinstance(t, int) else bass.DynSlice(t, 1)

        def rows(t):
            return slice(t * TB, (t + 1) * TB) if isinstance(t, int) else bass.DynSlice(t * TB, TB)

        def nth(t, u):
            return (t - u) * 8 + 16

        def iterations(eng, last, run):
            for t in range(4):
                run(t, t % 2)
            pairs = (last + 1 - 4) // 2
            with eng.Fori(0, pairs) as j:
                run(j * 2 + 4, 0)
                run(j * 2 + 5, 1)
            for t in range(4 + 2 * pairs, last + 1):
                run(t, t % 2)

        def there(t):
            return not isinstance(t, int) or 0 <= t < MT

        def expert_of(eng, t):
            return eng.value_load(routes.expert[0:1, one(t)], min_val=0, max_val=s.E - 1)

        def of_expert(tile, e):
            return tile[:, bass.DynSlice(e, 1), :].rearrange("p a n -> p (a n)")

        @block.sync
        def _(sp):
            def load(e):
                for n, dram in ((0, w1), (1, w2)):
                    expert = slice(e, e + 1) if isinstance(e, int) else bass.DynSlice(e, 1)
                    sp.dma_start(w_raw[n][:, expert, :].rearrange("p a (k f) -> p (a k) f", f=dram.shape[2]),
                                 dram[expert, :, :].rearrange("a (k p) f -> p (a k) f", p=P)).then_inc(w_loaded, 16)

            load(0)
            with sp.Fori(1, s.E) as e:
                sp.wait_ge(w_loaded, e * 32)
                load(e)
            sp.wait_ge(w_loaded, s.E * 32)

        @block.gpsimd
        def _(pool):
            g = nc.gpsimd
            g.memset(ones[:], 1.0).then_inc(tabs, 1)
            pool.wait_ge(tabs, 1)
            g.affine_select(out=ident[:], in_=ones[:], pattern=[[1, P]], compare_op=ALU.is_equal,
                            fill=0.0, base=0, channel_multiplier=-1).then_inc(tabs, 1)

            def collect(t, u):
                if late(t, 2):
                    pool.wait_ge(x_turned, t - 1)
                two = slice(t * HALVES, (t + 1) * HALVES) if isinstance(t, int) else bass.DynSlice(t * HALVES, HALVES)
                g.tensor_copy(token_t[:, u, :], routes.token[:, two]).then_inc(token_ready, 1)
                pool.wait_ge(token_ready, t + 1)
                pool.wait_ge(go, t + 1)
                g.tensor_tensor(go_tile[:], go_tile[:], go_tile[:], ALU.add).then_inc(go, 1)
                for h in range(HALVES):
                    g.indirect_dma_start(
                        out=x_t[:, u, h, :], out_offset=None, in_=y_dram,
                        in_offset=bass.IndirectOffsetOnAxis(ap=token_t[:, u, h:h + 1], axis=0),
                    ).then_inc(x_loaded[u], 16)

            def low(t, u):
                pool.wait_ge(hid_high_ready, t + 1)
                if late(t, 2):
                    pool.wait_ge(second_done, t - 1)
                g.tensor_tensor(hid_low[:, u, :, :], hid[:, u, :, :], hid_high[:, u, :, :].bitcast(F32),
                                ALU.subtract).then_inc(hid_low_ready, 1)

            g.memset(go_tile[:], 0.0).then_inc(go, 1)
            collect(0, 0)
            collect(1, 1)
            collect(2, 0)
            for t in range(2):
                collect(t + 3, 1 - t)
                low(t, t)
            with pool.Fori(1, MT // 2 - 2) as j:
                collect(j * 2 + 3, 1)
                low(j * 2, 0)
                collect(j * 2 + 4, 0)
                low(j * 2 + 1, 1)
            collect(MT - 1, 1)
            for t in range(MT - 4, MT):
                low(t, t % 2)

        @block.scalar
        def _(act):
            a = nc.scalar

            def weights(n, t, u):
                e = expert_of(act, t)
                act.wait_ge(w_loaded, e * 32 + 32)
                if late(t, 2):
                    act.wait_ge((first_done, second_done)[n], t - 1)
                a.activation(w_high[n][:, u, :], of_expert(w_raw[n], e), ACT.Copy).then_inc(w_high_ready[n], 1)

            def tokens(t, u):
                act.wait_ge(x_turned, t + 1)
                if late(t, 2):
                    act.wait_ge(first_done, t - 1)
                a.activation(x_high[:, u, :, :], ps_x[:, u, :, :], ACT.Copy).then_inc(x_high_ready, 1)

            def hidden(t, u):
                if late(t, 2):
                    act.wait_ge(hid_ready, (t - 1) * KF)
                    act.wait_ge(hid_low_ready, t - 1)
                a.activation(b1_t[:, u, :], routes.b1[:, one(t), :].rearrange("p a f -> p (a f)"),
                             ACT.Copy).then_inc(b1_ready, 1)
                act.wait_ge(b1_ready, t + 1)
                act.wait_ge(first_done, t + 1)
                for f in range(KF):
                    a.activation(hid[:, u, f, :], ps_h[:, u, f, :], ACT.Relu,
                                 bias=b1_t[:, u, f:f + 1]).then_inc(hid_ready, 1)

            def store(t, u):
                act.wait_ge(y_ready, (t + 1) * HALVES)
                act.dma_start(ys_dram[rows(t), :].rearrange("(h p) d -> p h d", p=P),
                              y_t[:, u, :, :]).then_inc(y_stored[u], 16)

            def load_b2(t, u):
                e = expert_of(act, t)
                if late(t, 2):
                    act.wait_ge(y_ready, (t - 1) * HALVES)
                act.dma_start(b2_t[:, u, :], b2[bass.DynSlice(e, 1), :].broadcast_to([P, D])).then_inc(b2_loaded[u], 16)

            def run(t, u):
                if there(t):
                    weights(1, t, u)
                if there(t + 1):
                    weights(0, t + 1, 1 - u)
                    tokens(t + 1, 1 - u)
                if there(t):
                    hidden(t, u)
                if there(t - 2):
                    store(t - 2, u)
                if there(t):
                    load_b2(t, u)

            weights(0, 0, 0)
            tokens(0, 0)
            iterations(act, MT - 2, run)
            for t in (MT - 1, MT, MT + 1):
                run(t, t % 2)
            for u in range(2):
                act.wait_ge(y_stored[u], 16 * (MT // 2))

        @block.vector
        def _(dve):
            v = nc.vector

            def weights(n, t, u):
                e = expert_of(dve, t)
                dve.wait_ge(w_high_ready[n], t + 1)
                v.tensor_tensor(w_low[n][:, u, :], of_expert(w_raw[n], e), w_high[n][:, u, :].bitcast(F32),
                                ALU.subtract).then_inc(w_low_ready[n], 1)

            def tokens(t, u):
                dve.wait_ge(x_high_ready, t + 1)
                v.tensor_tensor(x_low[:, u, :, :], ps_x[:, u, :, :], x_high[:, u, :, :].bitcast(F32),
                                ALU.subtract).then_inc(x_low_ready, 1)

            def hidden(t, u):
                dve.wait_ge(hid_ready, (t + 1) * KF)
                if late(t, 2):
                    dve.wait_ge(second_done, t - 1)
                    dve.wait_ge(hid_low_ready, t - 1)
                v.tensor_copy(hid_high[:, u, :, :], hid[:, u, :, :]).then_inc(hid_high_ready, 1)

            def result(t, u):
                dve.wait_ge(b2_loaded[u], nth(t, u))
                dve.wait_ge(second_done, t + 1)
                if late(t, 2):
                    dve.wait_ge(y_stored[u], nth(t, u) - 16)
                for h in range(HALVES):
                    v.tensor_tensor(y_t[:, u, h, :], ps_o[:, u, h, :], b2_t[:, u, :], ALU.add).then_inc(y_ready, 1)

            def run(t, u):
                if there(t):
                    weights(1, t, u)
                if there(t + 1):
                    weights(0, t + 1, 1 - u)
                    tokens(t + 1, 1 - u)
                if there(t):
                    hidden(t, u)
                if there(t - 1):
                    result(t - 1, 1 - u)

            weights(0, 0, 0)
            tokens(0, 0)
            iterations(dve, MT - 2, run)
            for t in (MT - 1, MT):
                run(t, t % 2)

        @block.tensor
        def _(pe):
            mm = nc.tensor.matmul

            def turn(t, u):
                pe.wait_ge(x_loaded[u], nth(t, u) * HALVES)
                if late(t, 2):
                    pe.wait_ge(x_low_ready, t - 1)
                for h in range(HALVES):
                    for k in range(KD):
                        ins = nc.tensor.transpose(ps_x[:, u, k, h * P:(h + 1) * P], x_t[:, u, h, k * P:(k + 1) * P],
                                                  ident[:, :])
                ins.then_inc(x_turned, 1)

            def first(t, u):
                pe.wait_ge(x_low_ready, t + 1)
                pe.wait_ge(w_low_ready[0], t + 1)
                if late(t, 2):
                    pe.wait_ge(hid_ready, (t - 1) * KF)
                for f in range(KF):
                    n = 0
                    for k in range(KD):
                        at = slice(k * F + f * P, k * F + (f + 1) * P)
                        for w, x in ((w_high, x_high), (w_high, x_low), (w_low, x_high)):
                            ins = mm(ps_h[:, u, f, :], w[0][:, u, at], x[:, u, k, :],
                                     start=(n == 0), stop=(n == 3 * KD - 1))
                            n += 1
                ins.then_inc(first_done, 1)

            def second(t, u):
                pe.wait_ge(hid_low_ready, t + 1)
                pe.wait_ge(w_low_ready[1], t + 1)
                if late(t, 2):
                    pe.wait_ge(y_ready, (t - 1) * HALVES)
                for half in range(HALVES):
                    n = 0
                    tokens = slice(half * P, (half + 1) * P)
                    for f in range(KF):
                        at = slice(f * D, (f + 1) * D)
                        for h, w in ((hid_high, w_high), (hid_high, w_low), (hid_low, w_high)):
                            ins = mm(ps_o[:, u, half, :], h[:, u, f, tokens], w[1][:, u, at],
                                     start=(n == 0), stop=(n == 3 * KF - 1))
                            n += 1
                ins.then_inc(second_done, 1)

            def run(t, u):
                if there(t + 1):
                    turn(t + 1, 1 - u)
                if there(t):
                    first(t, u)
                if there(t - 1):
                    second(t - 1, 1 - u)

            pe.wait_ge(tabs, 2)
            turn(0, 0)
            iterations(pe, MT - 2, run)
            for t in (MT - 1, MT):
                run(t, t % 2)


def phase_combine(nc, s, routes, gamma, x1_dram, y_dram, ys_dram, out):
    with ExitStack() as ctx:
        def sb(name, shape, dt=F32):
            return ctx.enter_context(nc.sbuf_tensor(name, shape, dt))

        def sem(name):
            return ctx.enter_context(nc.semaphore(name))

        CH, D = s.CH, s.D
        cuts = [0, 3] + [3 + (CH - 6) * n // 3 for n in (1, 2, 3)] + [CH]
        GROUPS = [range(a, b) for a, b in zip(cuts, cuts[1:])]
        NG = len(GROUPS)
        group_of = [g for g, cs in enumerate(GROUPS) for _ in cs]
        y = sb("y_again", [P, CH, D])
        x1 = sb("x1_again", [P, CH, D])
        found = sb("found", [P, CH, 2, D])
        gm = sb("gm", [P, D])
        stats = sb("stats_z", [P, CH, 6])
        mv = sb("mv_z", [P, CH, 2])
        std = sb("std_z", [P, CH])
        rstd = sb("rstd_z", [P, CH])
        fix = sb("fix_z", [P, CH])
        shift = sb("shift_z", [P, CH])

        gm_in = sem("gm_in")
        y_in = [sem(f"y_again_in_{g}") for g in range(NG)]
        x1_in = [sem(f"x1_again_in_{g}") for g in range(NG)]
        found_in = [[sem(f"found_{g}_{k}") for k in range(2)] for g in range(NG)]
        mixed = sem("mixed")
        stats_ready = sem("stats_z_ready")
        mv_ready = sem("mv_z_ready")
        std_ready = sem("std_z_ready")
        link_dve = sem("link_z")
        shift_ready = sem("shift_z_ready")
        normalised = sem("normalised")
        scaled = sem("scaled_z")
        done = sem("rows_done")
        stored = sem("rows_stored")

        block = ctx.enter_context(nc.Block())

        def rows(c):
            return P if c < s.FULL else s.REST

        @block.sync
        def _(sp):
            sp.dma_start(gm[:, :], gamma.rearrange("(a e) -> a e", a=1).broadcast_to([P, D])).then_inc(gm_in, 16)
            for g in range(NG):
                if g >= 2:
                    sp.wait_ge(found_in[g - 2][0], 16 * len(GROUPS[g - 2]))
                for dram, tile, into in ((y_dram, y, y_in), (x1_dram, x1, x1_in)):
                    full, tail = rows_of(dram, s)
                    cs = slice(GROUPS[g].start, min(GROUPS[g].stop, s.FULL))
                    sp.dma_start(tile[:, cs, :], full[:, cs, :]).then_inc(into[g], 16)
                    if g == NG - 1:
                        sp.dma_start(tile[0:s.REST, s.FULL, :], tail).then_inc(into[g], 16)
            for c in range(CH):
                sp.wait_ge(done, c + 1)
                sp.dma_start(out[c * P:c * P + rows(c), :], y[0:rows(c), c, :]).then_inc(stored, 16)
            sp.wait_ge(stored, 16 * CH)

        @block.gpsimd
        def _(pool):
            for c in range(CH):
                for k in range(2):
                    nc.gpsimd.indirect_dma_start(
                        out=found[0:rows(c), c, k, :], out_offset=None, in_=ys_dram,
                        in_offset=bass.IndirectOffsetOnAxis(
                            ap=routes.place[0:rows(c), k * CH + c:k * CH + c + 1], axis=0),
                    ).then_inc(found_in[group_of[c]][k], 16)

        @block.scalar
        def _(act):
            def normalise(g):
                act.wait_ge(shift_ready, g + 1)
                for c in GROUPS[g]:
                    n = rows(c)
                    nc.scalar.activation(y[0:n, c, :], y[0:n, c, :], ACT.Identity, bias=shift[0:n, c:c + 1],
                                         scale=rstd[0:n, c:c + 1]).then_inc(normalised, 1)

            for g in range(NG):
                act.wait_ge(mv_ready, g + 2)
                r = slice(GROUPS[g].start, GROUPS[g].stop)
                nc.scalar.activation(std[:, r], mv[:, r, 1], ACT.Sqrt).then_inc(std_ready, 1)
                normalise(g)

        @block.vector
        def _(dve):
            v = nc.vector
            n_link = [0]

            def link(ins):
                n_link[0] += 1
                ins.then_inc(link_dve, 1)
                dve.wait_ge(link_dve, n_link[0])

            v.memset(mv[:], 1.0).then_inc(mv_ready, 1)
            dve.wait_ge(mv_ready, 1)
            dve.wait_ge(gm_in, 16)

            def finish(g):
                dve.wait_ge(x1_in[g], 16 + 16 * (g == NG - 1))
                for c in GROUPS[g]:
                    n = rows(c)
                    dve.wait_ge(normalised, c + 1)
                    v.tensor_tensor(y[0:n, c, :], y[0:n, c, :], gm[0:n, :], ALU.mult).then_inc(scaled, 1)
                for c in GROUPS[g]:
                    n = rows(c)
                    dve.wait_ge(scaled, c + 1)
                    v.tensor_tensor(y[0:n, c, :], y[0:n, c, :], x1[0:n, c, :], ALU.add).then_inc(done, 1)

            n_mixed = 0
            for g in range(NG):
                cs, G = GROUPS[g], len(GROUPS[g])
                r = slice(cs.start, cs.stop)
                dve.wait_ge(y_in[g], 16 + 16 * (g == NG - 1))
                for k in range(2):
                    dve.wait_ge(found_in[g][k], 16 * G)
                    for c in cs:
                        n = rows(c)
                        if k:
                            dve.wait_ge(mixed, n_mixed - G + 1)
                        v.scalar_tensor_tensor(y[0:n, c, :], found[0:n, c, k, :], routes.weight[0:n, k, c:c + 1],
                                               y[0:n, c, :], ALU.mult, ALU.add).then_inc(mixed, 1)
                        n_mixed += 1
                for c in cs:
                    dve.wait_ge(mixed, n_mixed - G + (c - cs.start) + 1)
                    v.bn_stats(stats[0:rows(c), c, :], y[0:rows(c), c, :]).then_inc(stats_ready, 1)
                for c in cs:
                    dve.wait_ge(stats_ready, c + 1)
                    ins = v.bn_aggr(mv[0:rows(c), c, :], stats[0:rows(c), c, :])
                link(ins)
                v.tensor_scalar(mv[:, r, 1], mv[:, r, 1], 1e-5, None, ALU.add).then_inc(mv_ready, 1)
                dve.wait_ge(mv_ready, g + 2)
                dve.wait_ge(std_ready, g + 1)
                rsqrt(v, link, rstd[:, r], std[:, r], mv[:, r, 1], fix[:, r])
                link(v.tensor_tensor(rstd[:, r], rstd[:, r], fix[:, r], ALU.mult))
                v.scalar_tensor_tensor(shift[:, r], mv[:, r, 0], -1.0, rstd[:, r],
                                       ALU.mult, ALU.mult).then_inc(shift_ready, 1)
                if g:
                    finish(g - 1)
            finish(NG - 1)


class Tables:

    def __init__(self, nc, ctx, s, gather):
        def sb(name, shape, dt=F32):
            return ctx.enter_context(nc.sbuf_tensor(name, shape, dt))

        self.gather = gather
        self.lo_tab = sb("lo_tab", [P, P, s.BATCH], BF16)
        self.key_tab = sb("key_tab", [P, s.M, s.BATCH], BF16)
        self.key = sb("tab_key", [P, s.STEPS], BF16)
        self.lo = sb("tab_lo", [P, s.STEPS], BF16)
        self.w = [sb(f"tab_w{k}", [P, s.STEPS], BF16) for k in (1, 2)]
        self.w3 = sb("tab_w3", [P, s.STEPS])
        self.same = sb("tab_same", [P, s.STEPS])


def program(nc, x, src, dst, edge_weight, gate_w, gate_b, w1, b1, w2, b2, gamma, beta, out):
    s = Sizes(x.shape[0], x.shape[1], src.shape[0], gate_w.shape[1], w1.shape[2])
    a_dram = [nc.dram_tensor(f"a_{i}", [s.STEPS, s.CW * n, P], F32, kind="Internal").ap()
              for i, n in enumerate((s.CA, s.CB))]
    y_dram = nc.dram_tensor("tokens", [s.N, s.D], F32, kind="Internal").ap()
    x1_dram = nc.dram_tensor("x1_beta", [s.N, s.D], F32, kind="Internal").ap()
    ys_dram = nc.dram_tensor("results_sorted", [s.MT * s.TB, s.D], F32, kind="Internal").ap()
    with ExitStack() as ctx:
        routes = Routes(nc, ctx, s)
        with ExitStack() as nodes:
            x1, acc, hf = [nodes.enter_context(nc.sbuf_tensor(name, [P, s.CH, s.D], F32))
                           for name in ("x1", "acc", "hf")]
            moments = nodes.enter_context(nc.sbuf_tensor("moments", [P, s.CH, 6], F32))
            gather = nodes.enter_context(nc.sbuf_tensor("gather_rows", [P, s.CH], U32))
            with ExitStack() as stairs:
                tab = Tables(nc, stairs, s, gather)
                phase_tables(nc, s, x, src, dst, edge_weight, hf, acc, tab)
                phase_build(nc, s, tab, a_dram)
            phase_rounds(nc, s, gather, a_dram, acc, hf, x, x1, moments)
            y = acc
            phase_route(nc, s, moments, x1, y, gate_w, gate_b, b1, beta, routes, y_dram, x1_dram)
        phase_experts(nc, s, routes, w1, w2, b2, y_dram, ys_dram)
        phase_combine(nc, s, routes, gamma, x1_dram, y_dram, ys_dram, out)


NAMES = ["x", "src", "dst", "edge_weight", "L0_ffn_gate_w", "L0_ffn_gate_b", "L0_ffn_w1", "L0_ffn_b1",
         "L0_ffn_w2", "L0_ffn_b2", "L0_ffn_gamma", "L0_ffn_beta"]


def kernel(**inputs):
    import numpy as np
    import concourse.bacc as bacc
    from concourse.bass_utils import run_bass_kernel_spmd

    nc = bacc.Bacc("TRN2", target_bir_lowering=False, num_devices=1)
    arrays, aps = {}, []
    for name in NAMES:
        a = np.ascontiguousarray(inputs[name])
        arrays["in_" + name] = a
        aps.append(nc.dram_tensor("in_" + name, a.shape, mybir.dt.from_np(a.dtype), kind="ExternalInput").ap())
    out = nc.dram_tensor("out", inputs["x"].shape, F32, kind="ExternalOutput").ap()
    program(nc, *aps, out)
    result = run_bass_kernel_spmd(nc, [arrays], core_ids=[0])
    return result.results[0]["out"]
```
